# Optimizing a Trainium2 kernel written in Bass

```python
import numpy as np
import jax
import jax.numpy as jnp

def _softmax(x, axis=-1):
    return jax.nn.softmax(x, axis=axis)
def _gelu(x):
    return jax.nn.gelu(x, approximate=True)
def _silu(x):
    return jax.nn.silu(x)
def _sigmoid(x):
    return jax.nn.sigmoid(x)
def _layernorm(x, axis=-1, eps=1e-5):
    m = jnp.mean(x, axis=axis, keepdims=True)
    v = jnp.var(x, axis=axis, keepdims=True)
    return (x - m) / jnp.sqrt(v + eps)
def _scatter_add(tgt, idx, src, axis=0):
    return tgt.at[idx].add(src)
def _segment_sum(src, seg, n):
    return jax.ops.segment_sum(src, seg, n)

kernel_name = 'mk_conv_seq_d1_conv_nchw64_16dbcc'

def setup_inputs(seed: int = 0):
    np.random.seed(seed)
    _w = jnp.asarray
    def _rec_inputs():
        import jax
        import jax.numpy as jnp
        _gk = jax.random.key(seed)
        x = -0.0003482 + 1 * jax.random.normal(jax.random.fold_in(_gk, 1), (8, 64, 192, 192), jnp.float32)
        return x
    x = _rec_inputs()
    def _L0_conv_setup():
        import jax, jax.numpy as jnp
        import numpy as np
        MODES = 32
        NUM_BLOCKS = 4
        NUM_EXPERTS = 16
        TOP_K = 4
        TEMPERATURE = 2.0

        def _gelu(t):
            return jax.nn.gelu(t, approximate=False)

        def _c1(x, w, b):
            return jnp.einsum('bchw,oc->bohw', x, w) + b[None, :, None, None]

        def _group_norm(x, w, b, groups=8, eps=1e-05):
            B, C, H, W = x.shape
            xg = x.reshape(B, groups, C // groups, H, W)
            mu = xg.mean(axis=(2, 3, 4), keepdims=True)
            var = xg.var(axis=(2, 3, 4), keepdims=True)
            xn = ((xg - mu) * jax.lax.rsqrt(var + eps)).reshape(B, C, H, W)
            return xn * w[None, :, None, None] + b[None, :, None, None]

        def _bn_eval(x, g, b, rm, rv, eps=1e-05):
            return (x - rm) * jax.lax.rsqrt(rv + eps) * g + b

        def _afno(x, w1, b1, w2, b2):
            B, C, H, W = x.shape
            bs = C // NUM_BLOCKS
            xp = x.transpose(0, 2, 3, 1)
            xf = jnp.fft.rfft2(xp, axes=(1, 2), norm='ortho')
            Wf = xf.shape[2]
            xf = xf.reshape(B, H, Wf, NUM_BLOCKS, bs)
            m = MODES
            xm = xf[:, :m, :m]
            xr, xi = (xm.real, xm.imag)
            o1r = _gelu(jnp.einsum('bhwni,nio->bhwno', xr, w1[0]) - jnp.einsum('bhwni,nio->bhwno', xi, w1[1]) + b1[0])
            o1i = _gelu(jnp.einsum('bhwni,nio->bhwno', xi, w1[0]) + jnp.einsum('bhwni,nio->bhwno', xr, w1[1]) + b1[1])
            o2r = jnp.einsum('bhwni,nio->bhwno', o1r, w2[0]) - jnp.einsum('bhwni,nio->bhwno', o1i, w2[1]) + b2[0]
            o2i = jnp.einsum('bhwni,nio->bhwno', o1i, w2[0]) + jnp.einsum('bhwni,nio->bhwno', o1r, w2[1]) + b2[1]
            of = jnp.zeros((B, H, Wf, NUM_BLOCKS, bs), dtype=xf.dtype)
            of = of.at[:, :m, :m].set(o2r + 1j * o2i)
            out = jnp.fft.irfft2(of.reshape(B, H, Wf, C), s=(H, W), axes=(1, 2), norm='ortho')
            out = out + xp
            return out.transpose(0, 3, 1, 2)

        def _forward(x, gn1_w, gn1_b, afno_w1, afno_b1, afno_w2, afno_b2, gn2_w, gn2_b, fe_w, fe_b, g1_w, g1_b, bn1_g, bn1_b, bn1_rm, bn1_rv, ca_w1, ca_b1, ca_w2, ca_b2, g2_w, g2_b, bn2_g, bn2_b, bn2_rm, bn2_rv, g3_w, g3_b, shared_w, shared_b, expert_w, expert_b):
            residual = x
            h = _group_norm(x, gn1_w, gn1_b)
            h = _afno(h, afno_w1, afno_b1, afno_w2, afno_b2)
            h = h + residual
            residual = h
            h = _group_norm(h, gn2_w, gn2_b)
            feats = _gelu(_c1(h, fe_w, fe_b))
            shared = jnp.zeros_like(h)
            for s in range(shared_w.shape[0]):
                shared = shared + _gelu(_c1(feats, shared_w[s], shared_b[s])) / shared_w.shape[0]
            gf = feats.mean(axis=(2, 3))
            h1 = _gelu(_bn_eval(gf @ g1_w.T + g1_b, bn1_g, bn1_b, bn1_rm, bn1_rv))
            a = _gelu(h1 @ ca_w1.T + ca_b1) @ ca_w2.T + ca_b2
            h1 = h1 * jax.nn.sigmoid(2.0 * a)
            h2 = _gelu(_bn_eval(h1 @ g2_w.T + g2_b, bn2_g, bn2_b, bn2_rm, bn2_rv))
            scores = h2 @ g3_w.T + g3_b
            vals, idx = jax.lax.top_k(scores, TOP_K)
            wts = jax.nn.softmax(vals / TEMPERATURE, axis=1)
            B = x.shape[0]
            gate_w = jnp.zeros((B, NUM_EXPERTS), x.dtype).at[jnp.arange(B)[:, None], idx].add(wts)
            out = shared
            for e in range(NUM_EXPERTS):
                out = out + _gelu(_c1(feats, expert_w[e], expert_b[e])) * gate_w[:, e][:, None, None, None]
            return out + residual
        key = jax.random.key(seed)
        ks = jax.random.split(key, 16)
        B, C, H, W = (8, 64, 192, 192)
        nb = NUM_BLOCKS
        bs = C // nb
        E = NUM_EXPERTS
        scale = 1.0 / (bs * bs)
        f32 = jnp.float32
        n = lambda k, shape: jax.random.normal(k, shape, f32) * 0.02
        return {'x': jax.random.normal(ks[0], (B, C, H, W), f32), 'gn1_w': jnp.ones((C,), f32), 'gn1_b': jnp.zeros((C,), f32), 'afno_w1': jax.random.uniform(ks[1], (2, nb, bs, bs), f32) * scale, 'afno_b1': jax.random.uniform(ks[2], (2, nb, bs), f32) * scale, 'afno_w2': jax.random.uniform(ks[3], (2, nb, bs, bs), f32) * scale, 'afno_b2': jax.random.uniform(ks[4], (2, nb, bs), f32) * scale, 'gn2_w': jnp.ones((C,), f32), 'gn2_b': jnp.zeros((C,), f32), 'fe_w': n(ks[5], (C, C)), 'fe_b': jnp.zeros((C,), f32), 'g1_w': n(ks[6], (2 * C, C)), 'g1_b': jnp.zeros((2 * C,), f32), 'bn1_g': jnp.ones((2 * C,), f32), 'bn1_b': jnp.zeros((2 * C,), f32), 'bn1_rm': jnp.zeros((2 * C,), f32), 'bn1_rv': jnp.ones((2 * C,), f32), 'ca_w1': n(ks[7], (2 * C // 16, 2 * C)), 'ca_b1': jnp.zeros((2 * C // 16,), f32), 'ca_w2': n(ks[8], (2 * C, 2 * C // 16)), 'ca_b2': jnp.zeros((2 * C,), f32), 'g2_w': n(ks[9], (C, 2 * C)), 'g2_b': jnp.zeros((C,), f32), 'bn2_g': jnp.ones((C,), f32), 'bn2_b': jnp.zeros((C,), f32), 'bn2_rm': jnp.zeros((C,), f32), 'bn2_rv': jnp.ones((C,), f32), 'g3_w': n(ks[10], (E, C)), 'g3_b': jnp.zeros((E,), f32), 'shared_w': n(ks[11], (2, C, C)), 'shared_b': jnp.zeros((2, C), f32), 'expert_w': n(ks[12], (E, C, C)), 'expert_b': jnp.zeros((E, C), f32)}
    _L0_conv_all = _L0_conv_setup()
    _L0_conv_in = {k: v for k, v in _L0_conv_all.items() if k in ('gn1_w', 'gn1_b', 'afno_w1', 'afno_b1', 'afno_w2', 'afno_b2', 'gn2_w', 'gn2_b', 'fe_w', 'fe_b', 'g1_w', 'g1_b', 'bn1_g', 'bn1_b', 'bn1_rm', 'bn1_rv', 'ca_w1', 'ca_b1', 'ca_w2', 'ca_b2', 'g2_w', 'g2_b', 'bn2_g', 'bn2_b', 'bn2_rm', 'bn2_rv', 'g3_w', 'g3_b', 'shared_w', 'shared_b', 'expert_w', 'expert_b', )}
    del _L0_conv_all

    return {
        "x": x,
        "L0_conv_gn1_w": _L0_conv_in["gn1_w"],
        "L0_conv_gn1_b": _L0_conv_in["gn1_b"],
        "L0_conv_afno_w1": _L0_conv_in["afno_w1"],
        "L0_conv_afno_b1": _L0_conv_in["afno_b1"],
        "L0_conv_afno_w2": _L0_conv_in["afno_w2"],
        "L0_conv_afno_b2": _L0_conv_in["afno_b2"],
        "L0_conv_gn2_w": _L0_conv_in["gn2_w"],
        "L0_conv_gn2_b": _L0_conv_in["gn2_b"],
        "L0_conv_fe_w": _L0_conv_in["fe_w"],
        "L0_conv_fe_b": _L0_conv_in["fe_b"],
        "L0_conv_g1_w": _L0_conv_in["g1_w"],
        "L0_conv_g1_b": _L0_conv_in["g1_b"],
        "L0_conv_bn1_g": _L0_conv_in["bn1_g"],
        "L0_conv_bn1_b": _L0_conv_in["bn1_b"],
        "L0_conv_bn1_rm": _L0_conv_in["bn1_rm"],
        "L0_conv_bn1_rv": _L0_conv_in["bn1_rv"],
        "L0_conv_ca_w1": _L0_conv_in["ca_w1"],
        "L0_conv_ca_b1": _L0_conv_in["ca_b1"],
        "L0_conv_ca_w2": _L0_conv_in["ca_w2"],
        "L0_conv_ca_b2": _L0_conv_in["ca_b2"],
        "L0_conv_g2_w": _L0_conv_in["g2_w"],
        "L0_conv_g2_b": _L0_conv_in["g2_b"],
        "L0_conv_bn2_g": _L0_conv_in["bn2_g"],
        "L0_conv_bn2_b": _L0_conv_in["bn2_b"],
        "L0_conv_bn2_rm": _L0_conv_in["bn2_rm"],
        "L0_conv_bn2_rv": _L0_conv_in["bn2_rv"],
        "L0_conv_g3_w": _L0_conv_in["g3_w"],
        "L0_conv_g3_b": _L0_conv_in["g3_b"],
        "L0_conv_shared_w": _L0_conv_in["shared_w"],
        "L0_conv_shared_b": _L0_conv_in["shared_b"],
        "L0_conv_expert_w": _L0_conv_in["expert_w"],
        "L0_conv_expert_b": _L0_conv_in["expert_b"],
    }

def reference(x, L0_conv_gn1_w, L0_conv_gn1_b, L0_conv_afno_w1, L0_conv_afno_b1, L0_conv_afno_w2, L0_conv_afno_b2, L0_conv_gn2_w, L0_conv_gn2_b, L0_conv_fe_w, L0_conv_fe_b, L0_conv_g1_w, L0_conv_g1_b, L0_conv_bn1_g, L0_conv_bn1_b, L0_conv_bn1_rm, L0_conv_bn1_rv, L0_conv_ca_w1, L0_conv_ca_b1, L0_conv_ca_w2, L0_conv_ca_b2, L0_conv_g2_w, L0_conv_g2_b, L0_conv_bn2_g, L0_conv_bn2_b, L0_conv_bn2_rm, L0_conv_bn2_rv, L0_conv_g3_w, L0_conv_g3_b, L0_conv_shared_w, L0_conv_shared_b, L0_conv_expert_w, L0_conv_expert_b):
    import jax
    import jax.numpy as jnp
    def _L0_conv_ref(x, gn1_w, gn1_b, afno_w1, afno_b1, afno_w2, afno_b2, gn2_w, gn2_b, fe_w, fe_b, g1_w, g1_b, bn1_g, bn1_b, bn1_rm, bn1_rv, ca_w1, ca_b1, ca_w2, ca_b2, g2_w, g2_b, bn2_g, bn2_b, bn2_rm, bn2_rv, g3_w, g3_b, shared_w, shared_b, expert_w, expert_b):
        import jax, jax.numpy as jnp
        import numpy as np
        MODES = 32
        NUM_BLOCKS = 4
        NUM_EXPERTS = 16
        TOP_K = 4
        TEMPERATURE = 2.0

        def _gelu(t):
            return jax.nn.gelu(t, approximate=False)

        def _c1(x, w, b):
            return jnp.einsum('bchw,oc->bohw', x, w) + b[None, :, None, None]

        def _group_norm(x, w, b, groups=8, eps=1e-05):
            B, C, H, W = x.shape
            xg = x.reshape(B, groups, C // groups, H, W)
            mu = xg.mean(axis=(2, 3, 4), keepdims=True)
            var = xg.var(axis=(2, 3, 4), keepdims=True)
            xn = ((xg - mu) * jax.lax.rsqrt(var + eps)).reshape(B, C, H, W)
            return xn * w[None, :, None, None] + b[None, :, None, None]

        def _bn_eval(x, g, b, rm, rv, eps=1e-05):
            return (x - rm) * jax.lax.rsqrt(rv + eps) * g + b

        def _afno(x, w1, b1, w2, b2):
            B, C, H, W = x.shape
            bs = C // NUM_BLOCKS
            xp = x.transpose(0, 2, 3, 1)
            xf = jnp.fft.rfft2(xp, axes=(1, 2), norm='ortho')
            Wf = xf.shape[2]
            xf = xf.reshape(B, H, Wf, NUM_BLOCKS, bs)
            m = MODES
            xm = xf[:, :m, :m]
            xr, xi = (xm.real, xm.imag)
            o1r = _gelu(jnp.einsum('bhwni,nio->bhwno', xr, w1[0]) - jnp.einsum('bhwni,nio->bhwno', xi, w1[1]) + b1[0])
            o1i = _gelu(jnp.einsum('bhwni,nio->bhwno', xi, w1[0]) + jnp.einsum('bhwni,nio->bhwno', xr, w1[1]) + b1[1])
            o2r = jnp.einsum('bhwni,nio->bhwno', o1r, w2[0]) - jnp.einsum('bhwni,nio->bhwno', o1i, w2[1]) + b2[0]
            o2i = jnp.einsum('bhwni,nio->bhwno', o1i, w2[0]) + jnp.einsum('bhwni,nio->bhwno', o1r, w2[1]) + b2[1]
            of = jnp.zeros((B, H, Wf, NUM_BLOCKS, bs), dtype=xf.dtype)
            of = of.at[:, :m, :m].set(o2r + 1j * o2i)
            out = jnp.fft.irfft2(of.reshape(B, H, Wf, C), s=(H, W), axes=(1, 2), norm='ortho')
            out = out + xp
            return out.transpose(0, 3, 1, 2)

        def _forward(x, gn1_w, gn1_b, afno_w1, afno_b1, afno_w2, afno_b2, gn2_w, gn2_b, fe_w, fe_b, g1_w, g1_b, bn1_g, bn1_b, bn1_rm, bn1_rv, ca_w1, ca_b1, ca_w2, ca_b2, g2_w, g2_b, bn2_g, bn2_b, bn2_rm, bn2_rv, g3_w, g3_b, shared_w, shared_b, expert_w, expert_b):
            residual = x
            h = _group_norm(x, gn1_w, gn1_b)
            h = _afno(h, afno_w1, afno_b1, afno_w2, afno_b2)
            h = h + residual
            residual = h
            h = _group_norm(h, gn2_w, gn2_b)
            feats = _gelu(_c1(h, fe_w, fe_b))
            shared = jnp.zeros_like(h)
            for s in range(shared_w.shape[0]):
                shared = shared + _gelu(_c1(feats, shared_w[s], shared_b[s])) / shared_w.shape[0]
            gf = feats.mean(axis=(2, 3))
            h1 = _gelu(_bn_eval(gf @ g1_w.T + g1_b, bn1_g, bn1_b, bn1_rm, bn1_rv))
            a = _gelu(h1 @ ca_w1.T + ca_b1) @ ca_w2.T + ca_b2
            h1 = h1 * jax.nn.sigmoid(2.0 * a)
            h2 = _gelu(_bn_eval(h1 @ g2_w.T + g2_b, bn2_g, bn2_b, bn2_rm, bn2_rv))
            scores = h2 @ g3_w.T + g3_b
            vals, idx = jax.lax.top_k(scores, TOP_K)
            wts = jax.nn.softmax(vals / TEMPERATURE, axis=1)
            B = x.shape[0]
            gate_w = jnp.zeros((B, NUM_EXPERTS), x.dtype).at[jnp.arange(B)[:, None], idx].add(wts)
            out = shared
            for e in range(NUM_EXPERTS):
                out = out + _gelu(_c1(feats, expert_w[e], expert_b[e])) * gate_w[:, e][:, None, None, None]
            return out + residual
        return _forward(x, gn1_w, gn1_b, afno_w1, afno_b1, afno_w2, afno_b2, gn2_w, gn2_b, fe_w, fe_b, g1_w, g1_b, bn1_g, bn1_b, bn1_rm, bn1_rv, ca_w1, ca_b1, ca_w2, ca_b2, g2_w, g2_b, bn2_g, bn2_b, bn2_rm, bn2_rv, g3_w, g3_b, shared_w, shared_b, expert_w, expert_b)

    def _gn(v, G=32, eps=1e-5):
        B_, C_, H_, W_ = v.shape
        g = v.reshape(B_, G, C_ // G, H_, W_)
        m = jnp.mean(g, axis=(2, 3, 4), keepdims=True)
        s = jnp.var(g, axis=(2, 3, 4), keepdims=True)
        return ((g - m) / jnp.sqrt(s + eps)).reshape(v.shape)

    def _ln_c(v, eps=1e-6):
        m = jnp.mean(v, axis=1, keepdims=True)
        s = jnp.var(v, axis=1, keepdims=True)
        return (v - m) / jnp.sqrt(s + eps)

    def _ln_t(v, eps=1e-5):
        m = jnp.mean(v, axis=-1, keepdims=True)
        s = jnp.var(v, axis=-1, keepdims=True)
        return (v - m) / jnp.sqrt(s + eps)

    def _to_tokens(v):
        B_, C_, H_, W_ = v.shape
        return v.reshape(B_, C_, H_ * W_).transpose(0, 2, 1)
    def _from_tokens(t, like):
        B_, C_, H_, W_ = like.shape
        return t.transpose(0, 2, 1).reshape(B_, C_, H_, W_)

    x = _L0_conv_ref(x, L0_conv_gn1_w, L0_conv_gn1_b, L0_conv_afno_w1, L0_conv_afno_b1, L0_conv_afno_w2, L0_conv_afno_b2, L0_conv_gn2_w, L0_conv_gn2_b, L0_conv_fe_w, L0_conv_fe_b, L0_conv_g1_w, L0_conv_g1_b, L0_conv_bn1_g, L0_conv_bn1_b, L0_conv_bn1_rm, L0_conv_bn1_rv, L0_conv_ca_w1, L0_conv_ca_b1, L0_conv_ca_w2, L0_conv_ca_b2, L0_conv_g2_w, L0_conv_g2_b, L0_conv_bn2_g, L0_conv_bn2_b, L0_conv_bn2_rm, L0_conv_bn2_rv, L0_conv_g3_w, L0_conv_g3_b, L0_conv_shared_w, L0_conv_shared_b, L0_conv_expert_w, L0_conv_expert_b)
    return x


_drawn_inputs = setup_inputs


def setup_inputs(seed=0):
    import zlib

    import numpy as np

    out = dict(_drawn_inputs(seed))
    spreads = {'L0_conv_gn1_w': (1.0, 0.2),
     'L0_conv_gn1_b': (0.0, 0.1),
     'L0_conv_gn2_w': (1.0, 0.6),
     'L0_conv_gn2_b': (0.0, 0.8),
     'L0_conv_fe_b': (0.0, 0.8),
     'L0_conv_g1_b': (0.0, 0.8),
     'L0_conv_bn1_g': (1.0, 0.6),
     'L0_conv_bn1_b': (0.0, 2.0),
     'L0_conv_bn1_rm': (0.0, 0.8),
     'L0_conv_bn1_rv': (1.0, 0.6),
     'L0_conv_ca_b1': (0.0, 2.0),
     'L0_conv_ca_b2': (0.0, 0.8),
     'L0_conv_g2_b': (0.0, 2.0),
     'L0_conv_bn2_g': (1.0, 0.6),
     'L0_conv_bn2_b': (0.0, 2.0),
     'L0_conv_bn2_rm': (0.0, 0.8),
     'L0_conv_bn2_rv': (1.0, 0.6),
     'L0_conv_g3_b': (0.0, 0.594),
     'L0_conv_shared_b': (0.0, 0.564),
     'L0_conv_expert_b': (0.0, 0.626)}
    factors = {'L0_conv_afno_w1': 64.0,
     'L0_conv_afno_b1': 200.0,
     'L0_conv_afno_w2': 64.0,
     'L0_conv_afno_b2': 200.0,
     'L0_conv_fe_w': 8.0,
     'L0_conv_g1_w': 8.0,
     'L0_conv_ca_w1': 27.069,
     'L0_conv_ca_w2': 64.0,
     'L0_conv_g2_w': 8.0,
     'L0_conv_g3_w': 8.0,
     'L0_conv_shared_w': 8.0,
     'L0_conv_expert_w': 8.0}
    for name, (base, spread) in spreads.items():
        noise = np.random.default_rng([zlib.crc32(name.encode()), seed]).standard_normal(out[name].shape)
        drawn = base * np.exp(spread * noise) if base else spread * noise
        out[name] = jnp.asarray(drawn.astype(out[name].dtype))
    for name, factor in factors.items():
        out[name] = (out[name] * factor).astype(out[name].dtype)
    return out
```

```python
from contextlib import ExitStack

import numpy as np

import concourse.bass as bass
from concourse import mybir

F32 = mybir.dt.float32
I32 = mybir.dt.int32
ALU = mybir.AluOpType
ACT = mybir.ActivationFunctionType
AX = mybir.AxisListType

B, C, H, W = 8, 64, 192, 192
MODES = 32
NB = 4
BS = C // NB
E, TOPK = 16, 4
GROUPS = 8
GC = C // GROUPS
NPIX = H * W
EPS = 1e-5
P = 128
HH = H // 2
HW2 = HH * W
NM = MODES * MODES
KR = 2 * MODES

CG = 8
NG = C // CG
XT = 2 * CG * W
SLOTS = 4

UROW = 4
UPIX = UROW * W
UNITS = HH // UROW
BODY = 4
BODIES = UNITS // BODY
LROW = 2 * UROW
LPIX = LROW * W
BANK = 512
PAIR = 2 * BANK
STEP = 2 * PAIR
STEPS = HW2 // STEP
PAIRS = 2 * STEPS

OPEN = 16
TEMPERATURE = 2.0
G_DMAS = 8
CHAIN, GATE_CHAIN = 24, 14


def constants():
    k = np.arange(MODES)
    n = np.arange(H)
    ang = 2 * np.pi * np.outer(n, k) / H
    cos, sin = np.cos(ang), np.sin(ang)
    by = np.stack([cos, -sin], axis=-1).reshape(2, HH, KR).transpose(1, 0, 2)
    bx = (np.stack([cos, sin], axis=1) / H).reshape(2, HH, KR).transpose(1, 0, 2)
    iy = np.zeros((2, MODES, 2, H))
    iy[0, :, 0], iy[1, :, 0] = cos.T, -sin.T
    iy[0, :, 1], iy[1, :, 1] = sin.T, cos.T
    iy = np.tile(iy.reshape(KR, 2 * H), (2, 1))
    twice = np.where(k == 0, 1.0, 2.0)[:, None] / H
    ix = np.stack([cos.T * twice, -sin.T * twice], axis=1).reshape(KR, W)
    ix = np.tile(ix, (2, 1))
    ws = np.full((2, MODES, MODES), 2.0)
    ws[:, :, 0] = 0.5
    ws[0, 0, 0], ws[1, 0, 0] = 1.0, 0.0
    wx = np.full((2, MODES, MODES), 2.0)
    wx[:, :, 0] = 1.0
    wx[1, 0, 0] = 0.0
    ws = np.repeat(ws.reshape(2, NM), C, axis=0)
    wx = np.repeat(wx.reshape(2, NM), C, axis=0)
    c = np.arange(P)
    same = ((c[:, None] % C) // GC == (c[None, :] % C) // GC)
    grp_top = same * (c[:, None] < C)
    eye = np.eye(P)
    turn = np.zeros((P, P))
    turn[C + np.arange(C), np.arange(C)] = 1.0
    turn[np.arange(C), C + np.arange(C)] = -1.0
    top = (c < C)[:, None]
    e = np.arange(E)
    before = np.tile((e[None, :] < e[:, None]).reshape(1, E * E), (P, 1))
    slot = np.tile(np.repeat(np.arange(TOPK), E)[None, :], (P, 1))
    index = np.tile(e[None, :], (P, 1))
    named = dict(by=by.reshape(HH, 2 * KR), bx=bx.reshape(HH, 2 * KR), iy=iy, ix=ix, ws=ws, wx=wx,
                 grp_top=grp_top, grp_all=same, eye=eye, turn=turn, top=top, before=before, slot=slot,
                 index=index)
    return {"k_" + n: np.ascontiguousarray(a, dtype=np.float32) for n, a in named.items()}


def block_diagonal(a):
    n, m = a.shape
    out = np.zeros((2 * n, 2 * m), a.dtype)
    out[:n, :m] = a
    out[n:, m:] = a
    return out


def laid_out(i):
    g = {k.removeprefix("L0_conv_"): np.asarray(v) for k, v in i.items()}

    def twice(v):
        return np.tile(v.reshape(-1, 1), (2, 1))

    def afno(w):
        full = np.zeros((2, C, 2, C), w.dtype)
        for n in range(NB):
            s = slice(n * BS, (n + 1) * BS)
            full[0, s, 0, s] = w[0, n]
            full[0, s, 1, s] = w[1, n]
            full[1, s, 0, s] = w[1, n]
            full[1, s, 1, s] = w[0, n]
        return full.reshape(P, P)

    experts = np.zeros((E, P, P + 1), g["expert_w"].dtype)
    for e in range(E):
        experts[e, :, :P] = block_diagonal(g["expert_w"][e].T)
        experts[e, :, P] = np.tile(g["expert_b"][e], 2)
    cols = [twice(g[n]) for n in ("gn1_w", "gn1_b", "gn2_w", "gn2_b", "fe_b")]
    cols += [twice(g["shared_b"][s]) for s in range(2)]
    cols += [g["afno_b1"].reshape(P, 1), g["afno_b2"].reshape(P, 1)]
    cols += [g[n].reshape(P, 1) for n in ("g1_b", "bn1_g", "bn1_b", "bn1_rm", "bn1_rv", "ca_b2")]
    pad = lambda v: np.concatenate([v.reshape(-1, 1), np.ones((P - v.size, 1), v.dtype)])
    cols += [pad(g[n]) for n in ("ca_b1", "g2_b", "bn2_g", "bn2_b", "bn2_rm", "bn2_rv")]
    return dict(
        x=g["x"],
        p_cols=np.concatenate(cols, axis=1),
        p_fe=block_diagonal(g["fe_w"].T), p_sh0=block_diagonal(g["shared_w"][0].T),
        p_sh1=block_diagonal(g["shared_w"][1].T), p_w1=afno(g["afno_w1"]), p_w2=afno(g["afno_w2"]),
        p_g1=np.tile(g["g1_w"].T, (2, 1)), p_ca1=g["ca_w1"].T, p_ca2=g["ca_w2"].T, p_g2=g["g2_w"].T,
        p_g3=g["g3_w"].T, p_g3b=np.tile(g["g3_b"].reshape(1, E), (P, 1)), p_experts=experts,
    )


(GN1W, GN1B, GN2W, GN2B, FEB, SB0, SB1, AB1, AB2, G1B, BN1G, BN1B, BN1RM, BN1RV, CAB2,
 CAB1, G2B, BN2G, BN2B, BN2RM, BN2RV) = range(21)


def build(nc, d, out):
    ctx = ExitStack()
    with ctx:
        def sb(name, shape, dt=F32):
            return ctx.enter_context(nc.sbuf_tensor(name, shape, dt))

        def sem(name):
            return ctx.enter_context(nc.semaphore(name))

        g_dram = nc.dram_tensor("g_scratch", [B, 2, KR, C, HH], F32, kind="Internal").ap()

        big_h = sb("big_h", [P, HW2])
        big_f = sb("big_f", [P, HW2])
        g_all = sb("g_all", [P, C, HH])
        g_row = sb("g_row", [P, 2, UROW, C])
        y_buf = sb("y_buf", [P, 2, PAIR])
        con = {}
        for name, width in (("by", 2 * KR), ("bx", 2 * KR), ("iy", 2 * H), ("ix", W), ("grp_top", P), ("grp_all", P),
                            ("eye", P), ("turn", P), ("top", 1), ("before", E * E), ("slot", TOPK * E),
                            ("index", E)):
            con[name] = sb("c_" + name, [HH if name in ("by", "bx") else P, width])
        par = {}
        for name, rows, width in (("cols", P, 21), ("fe", P, P), ("sh0", P, P), ("sh1", P, P), ("w1", P, P), ("w2", P, P),
                                  ("g1", P, P), ("ca1", P, E // 2), ("ca2", E // 2, P), ("g2", P, C), ("g3", C, E), ("g3b", P, E)):
            par[name] = sb("w_" + name, [rows, width])
        fe_all = sb("fe_all", [P, B, P])
        fe_b = sb("fe_b", [P, P])
        febias = sb("febias", [P, B])
        alpha = sb("alpha", [P, B])
        w_sel = sb("w_sel", [P, TOPK, P + 1])
        ones = sb("ones", [P, 1])
        mhalf = sb("mhalf", [P, 2])
        sq_cg = sb("sq_cg", [HH, 2, C])
        sq_dup = sb("sq_dup", [HH, 2, C])
        st = sb("st", [P, 32])
        bn = sb("bn", [P, 12])
        gf_parts = sb("gf_parts", [P, UNITS])
        gt = sb("gt", [P, 16])
        h2_wide = sb("h2_wide", [C, P])
        sc = sb("sc", [P, E])
        cmp_a = sb("cmp_a", [P, E, E])
        cmp_b = sb("cmp_b", [P, E, E])
        rank = sb("rank", [P, E])
        pick = sb("pick", [P, TOPK, E])
        picked = sb("picked", [P, TOPK, E])
        val = sb("val", [P, TOPK])
        ex = sb("ex", [P, TOPK])
        gate = sb("gate", [P, TOPK])
        idxf = sb("idxf", [P, TOPK])
        idx = sb("idx", [P, TOPK], I32)

        ps = ctx.enter_context(nc.psum_tensor("ps", [P, 8, BANK], F32))

        xt = [big_h[0:HH, s * XT:(s + 1) * XT].rearrange("p (h c x) -> p h c x", h=2, c=CG) for s in range(SLOTS)]
        sq = big_h[0:HH, SLOTS * XT:(SLOTS + 1) * XT].rearrange("p (h c x) -> p h c x", h=2, c=CG)
        g_st = [big_h[:, (SLOTS + 1) * XT + s * 4 * H:(SLOTS + 1) * XT + (s + 1) * 4 * H].rearrange("p (k r y) -> p k r y", k=2, r=2)
                for s in range(2)]
        tt = big_f[0:HH, 0:2 * KR * C].rearrange("p (h k c) -> p h k c", h=2, k=KR)
        o = 2 * KR * C
        p_modes = big_f[:, o:o + 2 * NM].rearrange("p (k t q) -> p k t q", k=MODES, t=2)
        x_modes, h_modes, o1, s_modes, tmp1, st_modes = (big_f[:, o + n * NM:o + (n + 1) * NM] for n in range(2, 8))
        wgt_s, wgt_x = y_buf[:, 0, :], y_buf[:, 1, :]
        st_v = st_modes.rearrange("p (k c) -> p k c", c=C)

        s_const = sem("const_loaded")
        s_setup, s_bnvar, s_bnrstd = sem("setup_chain"), sem("bn_var_ready"), sem("bn_rstd_ready")
        s_ready, s_half = sem("setup_done"), sem("exponent_ready")
        s_passed, s_gfree = sem("wait_passed"), sem("g_staging_free")
        s_xt = [sem(f"xt_loaded{s}") for s in range(SLOTS)]
        s_gst = [sem(f"g_stored{s}") for s in range(2)]
        s_f1, s_tt, s_square, s_reduced = sem("f1_done"), sem("t_written"), sem("squared"), sem("squares_reduced")
        s_f2, s_pm, s_x = sem("f2_done"), sem("p_written"), sem("x_done")
        s_stat, s_sums, s_var, s_rstd = sem("stats_ready"), sem("sums_done"), sem("variance_ready"), sem("rstd_ready")
        s_hm, s_w1, s_o1, s_w2, s_s = sem("h_modes_ready"), sem("w1_done"), sem("o1_written"), sem("w2_done"), sem("s_written")
        s_st, s_stw, s_g, s_gw = sem("st_done"), sem("st_written"), sem("g_done"), sem("g_written")
        s_nb2, s_fs, s_spec, s_chain = sem("shift2_ready"), sem("fe_shift_done"), sem("batch_modes_done"), sem("dve_chain")
        s_xl = [sem(f"x_loaded{s}") for s in range(2)]
        s_gall, s_grow, s_par = sem("g_loaded"), sem("g_rows_written"), sem("batch_weights_ready")
        s_srow, s_h, s_fe, s_feat = sem("s_rows_done"), sem("h_written"), sem("fe_done"), sem("feats_written")
        s_sh, s_shy, s_sacc = sem("shared_done"), sem("shared_gelu_done"), sem("shared_added")
        s_mm, s_ga, s_gd, s_exp = sem("gate_matmul_done"), sem("gate_act_done"), sem("gate_dve_done"), sem("gate_exp_done")
        s_gchain, s_top, s_idx, s_wsel = sem("gate_chain"), sem("gate_max_ready"), sem("indices_ready"), sem("experts_loaded")
        s_ex, s_exy, s_eacc, s_store = sem("expert_done"), sem("expert_gelu_done"), sem("expert_added"), sem("out_stored")
        block = ctx.enter_context(nc.Block())

        x_y = d["x"].rearrange("b (g c) (h y) w -> (b g) h y c w", g=NG, h=2)
        x_c = d["x"].rearrange("b c (h y) w -> b h c (y w)", h=2)
        out_c = out.rearrange("b c (h y) w -> b h c (y w)", h=2)
        CONSTS = (len(con) + len(par) + 2) * 16
        col = lambda n: par["cols"][:, n:n + 1]

        def alone(eng):
            eng.sem_inc(s_passed, 1)

        @block.sync
        def _(sp):
            sp.sem_inc(s_store, 16 * OPEN)
            for name, t in con.items():
                sp.dma_start(t[:, :], d["k_" + name]).then_inc(s_const, 16)
            for name, t in par.items():
                sp.dma_start(t[:, :], d["p_" + name]).then_inc(s_const, 16)
            sp.dma_start(wgt_s, d["k_ws"]).then_inc(s_const, 16)
            sp.dma_start(wgt_x, d["k_wx"]).then_inc(s_const, 16)

            with sp.Fori(0, B * NG // SLOTS) as r:
                for s in range(SLOTS):
                    sp.wait_ge(s_f1, OPEN + r * SLOTS + s - SLOTS + 1)
                    alone(sp)
                    sp.wait_ge(s_square, OPEN + r * SLOTS + s - SLOTS + 1)
                    alone(sp)
                    for h in range(2):
                        sp.dma_start(xt[s][:, h], x_y[bass.ds(r * SLOTS + s, 1), h].rearrange("q y c w -> (q y) c w"))\
                          .then_inc(s_xt[s], 16)

            sp.wait_ge(s_spec, OPEN + B)
            for s in range(2):
                sp.wait_ge(s_gst[s], B * 4 * G_DMAS * 16)

            def load_x(b, l, s):
                for h in range(2):
                    sp.dma_start(big_h[h * C:(h + 1) * C, bass.ds(l * LPIX, LPIX)],
                                 x_c[bass.ds(b, 1), h, :, bass.ds(l * LPIX, LPIX)].rearrange("b c n -> (b c) n"))\
                      .then_inc(s_xl[s], 16)

            def load_g(b):
                for h in range(2):
                    sp.dma_start(g_all[h * KR:(h + 1) * KR], g_dram[bass.ds(b, 1), h].rearrange("b m c y -> (b m) c y"))\
                      .then_inc(s_gall, 16)

            def store(b, n):
                sp.wait_ge(s_eacc, OPEN + (b * PAIRS + (n + 1) * 2) * TOPK)
                alone(sp)
                sp.wait_ge(s_store, 16 * OPEN + (b * STEPS + n) * 32)
                alone(sp)
                for h in range(2):
                    sp.dma_start(out_c[bass.ds(b, 1), h, :, bass.ds(n * STEP, STEP)].rearrange("b c n -> (b c) n"),
                                 big_h[h * C:(h + 1) * C, bass.ds(n * STEP, STEP)]).then_inc(s_store, 16)

            def batch(b, last):
                with sp.Fori(1, BODIES) as r:
                    for l in range(2):
                        sp.wait_ge(s_h, OPEN + b * UNITS + (r - 1) * BODY + 2 * l + 2)
                        alone(sp)
                        load_x(b, r * 2 + l, l)
                sp.wait_ge(s_idx, b + 1)
                alone(sp)
                for k in range(TOPK):
                    e = sp.value_load(idx[0:1, k:k + 1], min_val=0, max_val=E - 1)
                    sp.dma_start(w_sel[:, k], d["p_experts"][bass.ds(e, 1)].rearrange("e p n -> (e p) n")).then_inc(s_wsel, 16)
                for n in range(2):
                    store(b, n)
                if not last:
                    sp.wait_ge(s_grow, (b + 1) * UNITS)
                    alone(sp)
                    load_g(b + 1)
                    sp.wait_ge(s_store, 16 * OPEN + (b * STEPS + 2) * 32)
                    alone(sp)
                    for l in range(2):
                        load_x(b + 1, l, l)
                with sp.Fori(2, STEPS) as n:
                    store(b, n)
                sp.wait_ge(s_store, 16 * OPEN + (b + 1) * STEPS * 32)
                alone(sp)

            load_g(0)
            for l in range(2):
                load_x(0, l, l)
            with sp.Fori(0, B - 1) as b:
                batch(b, False)
            batch(B - 1, True)

        @block.tensor
        def _(pe):
            mm = nc.tensor.matmul
            pe.wait_ge(s_const, CONSTS)
            pe.wait_ge(s_ready, 1)
            pe.sem_inc(s_f1, OPEN)
            pe.sem_inc(s_f2, OPEN)
            pe.sem_inc(s_srow, OPEN)

            with pe.Fori(0, B) as b:
                pe.wait_ge(s_gw, OPEN + b * 8)
                for q in range(NG):
                    s = q % SLOTS
                    pe.wait_ge(s_xt[s], (b * 2 + q // SLOTS + 1) * 32)
                    pe.wait_ge(s_tt, OPEN + b * NG + q - 1)
                    for c in range(CG):
                        for xc in range(2):
                            for h in range(2):
                                i = mm(ps[0:HH, 2 * (s % 2) + xc, c * KR:(c + 1) * KR], xt[s][:, h, c, xc * HH:(xc + 1) * HH],
                                       con["by"][:, h * KR:(h + 1) * KR], start=(h == 0), stop=(h == 1))
                    i.then_inc(s_f1, 1)
                pe.wait_ge(s_tt, OPEN + (b + 1) * NG)
                pe.wait_ge(s_spec, OPEN + b)
                for ky in range(MODES):
                    for xc in range(2):
                        i = mm(ps[:, 4 + ky // 8, (ky % 8) * KR:(ky % 8 + 1) * KR],
                               tt[:, xc, 2 * ky:2 * ky + 2, :].rearrange("p k c -> p (k c)"),
                               con["bx"][:, xc * KR:(xc + 1) * KR], start=(xc == 0), stop=(xc == 1))
                i.then_inc(s_f2, 1)
                pe.wait_ge(s_pm, b + 1)
                for half in range(2):
                    k = slice(half * 16, half * 16 + 16)
                    mm(ps[:, 4 + half, :], con["eye"][:, :], p_modes[:, k, 0, :], start=True, stop=False)
                    i = mm(ps[:, 4 + half, :], con["turn"][:, :], p_modes[:, k, 1, :], start=False, stop=True)
                i.then_inc(s_x, 1)
                pe.wait_ge(s_stat, 3 * b + 1)
                mm(ps[:, 6, 0:1], sq_dup[:, :, :].rearrange("p a c -> p (a c)"), ones[0:HH, :], start=True, stop=True)\
                    .then_inc(s_sums, 1)
                pe.wait_ge(s_stat, 3 * b + 2)
                mm(ps[:, 6, 2:4], con["grp_top"][:, :], st[:, 0:2], start=True, stop=True).then_inc(s_sums, 1)
                pe.wait_ge(s_hm, b + 1)
                for half in range(2):
                    i = mm(ps[:, 4 + half, :], par["w1"][:, :], h_modes[:, half * BANK:(half + 1) * BANK], start=True, stop=True)
                i.then_inc(s_w1, 1)
                pe.wait_ge(s_o1, b + 1)
                for half in range(2):
                    i = mm(ps[:, 6 + half, :], par["w2"][:, :], o1[:, half * BANK:(half + 1) * BANK], start=True, stop=True)
                i.then_inc(s_w2, 1)
                pe.wait_ge(s_s, b + 1)
                alone(pe)
                s_k = s_modes.rearrange("p (ky kx) -> p kx ky", ky=MODES)
                for kx in range(MODES):
                    for ri in range(2):
                        p0 = (kx % 2) * KR + ri * MODES
                        n = kx // 2
                        rows = slice(ri * C, (ri + 1) * C)
                        i = mm(ps[p0:p0 + MODES, 4 + n // 8, (n % 8) * C:(n % 8 + 1) * C], s_k[rows, kx, :],
                               con["eye"][rows, rows], start=True, stop=True)
                i.then_inc(s_st, 1)
                pe.wait_ge(s_stat, 3 * b + 3)
                mm(ps[:, 6, 0:2], con["grp_all"][:, :], st[:, 16:18], start=True, stop=True).then_inc(s_sums, 1)
                pe.wait_ge(s_stw, b + 1)
                alone(pe)
                for n in range(MODES // 2):
                    if n % 2 == 0 and n >= 4:
                        pe.wait_ge(s_gw, OPEN + b * 8 + n // 2 - 1)
                        alone(pe)
                    for odd in range(2):
                        r = slice(odd * KR, (odd + 1) * KR)
                        i = mm(ps[odd * C:(odd + 1) * C, (4, 5, 0, 1)[n % 4], 0:2 * H], st_v[r, n, :], con["iy"][r, :],
                               start=True, stop=True)
                    if n % 2 == 1:
                        i.then_inc(s_g, 1)
                pe.wait_ge(s_nb2, b + 1)
                mm(ps[:, 6, 4:5], par["fe"][:, :], st[:, 20:21], start=True, stop=True).then_inc(s_fs, 1)

            def srows(b, u, j):
                pe.wait_ge(s_grow, b * UNITS + u + 1)
                pe.wait_ge(s_h, OPEN + b * UNITS + u)
                alone(pe)
                for r in range(UROW):
                    for h in range(2):
                        k = slice(h * C, (h + 1) * C)
                        i = mm(ps[k, r // 2, (r % 2) * W:(r % 2 + 1) * W], g_row[k, j % 2, r, :], con["ix"][k, :],
                               start=True, stop=True)
                i.then_inc(s_srow, 1)

            def fe(b, u):
                pe.wait_ge(s_h, OPEN + b * UNITS + u + 1)
                pe.wait_ge(s_feat, OPEN + b * UNITS + u)
                for half in range(2):
                    i = mm(ps[:, 2 + half, 0:2 * W], fe_b[:, :], big_h[:, bass.ds(u * UPIX + half * 2 * W, 2 * W)],
                           start=True, stop=True)
                i.then_inc(s_fe, 1)

            def shared(b, u):
                pe.wait_ge(s_feat, OPEN + b * UNITS + u + 1)
                for k in range(2):
                    pe.wait_ge(s_shy, OPEN + (b * UNITS + u - 1) * 2 + k + 1)
                    for half in range(2):
                        i = mm(ps[:, 4 + 2 * k + half, 0:2 * W], par[f"sh{k}"][:, :],
                               big_f[:, bass.ds(u * UPIX + half * 2 * W, 2 * W)], start=True, stop=True)
                    i.then_inc(s_sh, 1)

            def expert(b, p):
                for k in range(TOPK):
                    pe.wait_ge(s_exy, OPEN + (b * PAIRS + p - 1) * TOPK + k + 1)
                    for half in range(2):
                        i = mm(ps[:, 2 * k + half, :], w_sel[:, k, 0:P], big_f[:, bass.ds(p * PAIR + half * BANK, BANK)],
                               start=True, stop=True)
                    i.then_inc(s_ex, 1)

            pe.wait_ge(s_gw, OPEN + B * 8)
            with pe.Fori(0, B) as b:
                pe.wait_ge(s_par, b + 1)
                pe.wait_ge(s_exy, OPEN + b * PAIRS * TOPK)
                for j in range(BODY):
                    srows(b, j, j)
                    if j:
                        shared(b, j - 1)
                    fe(b, j)
                with pe.Fori(1, BODIES) as r:
                    for j in range(BODY):
                        srows(b, r * BODY + j, j)
                        shared(b, r * BODY + j - 1)
                        fe(b, r * BODY + j)
                shared(b, UNITS - 1)
                pe.wait_ge(s_gd, 2 * b + 1)
                mm(ps[:, 0, 0:1], par["g1"][:, :], gt[:, 0:1], start=True, stop=True).then_inc(s_mm, 1)
                pe.wait_ge(s_ga, 5 * b + 1)
                mm(ps[0:E // 2, 0, 1:2], par["ca1"][:, :], gt[:, 1:2], start=True, stop=True).then_inc(s_mm, 1)
                pe.wait_ge(s_ga, 5 * b + 2)
                mm(ps[:, 0, 2:3], par["ca2"][:, :], gt[0:E // 2, 2:3], start=True, stop=True).then_inc(s_mm, 1)
                pe.wait_ge(s_gd, 2 * b + 2)
                mm(ps[0:C, 0, 3:4], par["g2"][:, :], gt[:, 4:5], start=True, stop=True).then_inc(s_mm, 1)
                pe.wait_ge(s_ga, 5 * b + 5)
                mm(ps[:, 0, 8:8 + E], h2_wide[:, :], par["g3"][:, :], start=True, stop=True).then_inc(s_mm, 1)
                pe.wait_ge(s_wsel, (b + 1) * TOPK * 16)
                pe.wait_ge(s_shy, OPEN + (b + 1) * UNITS * 2)
                alone(pe)
                with pe.Fori(0, STEPS) as n:
                    for j in range(2):
                        expert(b, n * 2 + j)

        @block.scalar
        def _(act):
            a = nc.scalar.activation
            act.wait_ge(s_const, CONSTS)
            act.wait_ge(s_ready, 1)
            act.sem_inc(s_square, OPEN)
            act.sem_inc(s_tt, OPEN)
            act.sem_inc(s_gw, OPEN)
            act.sem_inc(s_feat, OPEN)
            act.sem_inc(s_shy, OPEN)
            act.sem_inc(s_exy, OPEN)

            with act.Fori(0, B) as b:
                for q in range(NG):
                    s = q % SLOTS
                    act.wait_ge(s_xt[s], (b * 2 + q // SLOTS + 1) * 32)
                    act.wait_ge(s_reduced, OPEN + b * NG + q)
                    a(sq, xt[s], ACT.Square).then_inc(s_square, 1)
                    act.wait_ge(s_f1, OPEN + b * NG + q + 1)
                    act.wait_ge(s_f2, OPEN + b)
                    src = ps[0:HH, 2 * (s % 2):2 * (s % 2) + 2, :].rearrange("p h (c k) -> p h k c", c=CG)
                    for xc in range(2):
                        i = a(tt[:, xc, :, q * CG:(q + 1) * CG], src[:, xc], ACT.Copy)
                    i.then_inc(s_tt, 1)
                act.wait_ge(s_f2, OPEN + b + 1)
                a(p_modes.rearrange("p k t q -> p (k t q)").rearrange("p (a n) -> p a n", a=4), ps[:, 4:8, :], ACT.Copy)\
                    .then_inc(s_pm, 1)
                act.wait_ge(s_w1, b + 1)
                a(o1.rearrange("p (a n) -> p a n", a=2), ps[:, 4:6, :], ACT.Gelu, bias=col(AB1)).then_inc(s_o1, 1)
                act.wait_ge(s_st, b + 1)
                a(st_modes.rearrange("p (a n) -> p a n", a=2), ps[:, 4:6, :], ACT.Copy).then_inc(s_stw, 1)
                for n in range(8):
                    act.wait_ge(s_g, b * 8 + n + 1)
                    act.wait_ge(s_gfree, OPEN + b * 8 + n - 1)
                    bank = (4, 0)[n % 2]
                    a(g_st[n % 2].rearrange("p k r y -> p k (r y)"), ps[:, bank:bank + 2, 0:2 * H], ACT.Copy).then_inc(s_gw, 1)

            def feats(b, u):
                act.wait_ge(s_fe, b * UNITS + u + 1)
                a(big_f[:, bass.ds(u * UPIX, UPIX)].rearrange("p (a n) -> p a n", a=2), ps[:, 2:4, 0:2 * W], ACT.Gelu,
                  bias=gt[:, 10:11], accum_out=gf_parts[:, bass.ds(u, 1)]).then_inc(s_feat, 1)

            def shared_gelu(b, u):
                for k in range(2):
                    act.wait_ge(s_sh, (b * UNITS + u) * 2 + k + 1)
                    act.wait_ge(s_sacc, OPEN + (b * UNITS + u - 1) * 2 + k + 1)
                    a(y_buf[:, k, 0:UPIX].rearrange("p (a n) -> p a n", a=2), ps[:, 4 + 2 * k:6 + 2 * k, 0:2 * W], ACT.Gelu,
                      bias=col(SB0 + k)).then_inc(s_shy, 1)

            def expert_gelu(b, p):
                for k in range(TOPK):
                    act.wait_ge(s_ex, (b * PAIRS + p) * TOPK + k + 1)
                    act.wait_ge(s_eacc, OPEN + (b * PAIRS + p) * TOPK + k - 1)
                    a(y_buf[:, k % 2, :].rearrange("p (a n) -> p a n", a=2), ps[:, 2 * k:2 * k + 2, :], ACT.Gelu,
                      bias=w_sel[:, k, P:P + 1]).then_inc(s_exy, 1)

            act.wait_ge(s_spec, OPEN + B)
            with act.Fori(0, B) as b:
                act.wait_ge(s_par, b + 1)
                act.wait_ge(s_eacc, OPEN + b * PAIRS * TOPK)
                for j in range(BODY):
                    if j:
                        shared_gelu(b, j - 1)
                    feats(b, j)
                with act.Fori(1, BODIES) as r:
                    for j in range(BODY):
                        shared_gelu(b, r * BODY + j - 1)
                        feats(b, r * BODY + j)
                shared_gelu(b, UNITS - 1)
                act.wait_ge(s_mm, 5 * b + 1)
                a(gt[:, 1:2], ps[:, 0, 0:1], ACT.Gelu, bias=bn[:, 1:2], scale=bn[:, 2:3]).then_inc(s_ga, 1)
                act.wait_ge(s_mm, 5 * b + 2)
                a(gt[0:E // 2, 2:3], ps[0:E // 2, 0, 1:2], ACT.Gelu, bias=par["cols"][0:E // 2, CAB1:CAB1 + 1])\
                    .then_inc(s_ga, 1)
                act.wait_ge(s_mm, 5 * b + 3)
                a(gt[:, 3:4], ps[:, 0, 2:3], ACT.Sigmoid, bias=bn[:, 3:4], scale=2.0).then_inc(s_ga, 1)
                act.wait_ge(s_mm, 5 * b + 4)
                a(gt[0:C, 5:6], ps[0:C, 0, 3:4], ACT.Gelu, bias=bn[0:C, 5:6], scale=bn[0:C, 4:5]).then_inc(s_ga, 1)
                act.wait_ge(s_ga, 5 * b + 4)
                a(h2_wide[:, :], con["eye"][0:C, :], ACT.Identity, bias=gt[0:C, 5:6], scale=0.0).then_inc(s_ga, 1)
                act.wait_ge(s_top, b + 1)
                a(ex[:, :], val[:, :], ACT.Exp, bias=gt[:, 6:7], scale=1.0 / TEMPERATURE, accum_out=gt[:, 7:8])\
                    .then_inc(s_exp, 1)
                act.wait_ge(s_wsel, (b + 1) * TOPK * 16)
                act.wait_ge(s_sacc, OPEN + (b + 1) * UNITS * 2)
                alone(act)
                with act.Fori(0, STEPS) as n:
                    for j in range(2):
                        expert_gelu(b, n * 2 + j)

        @block.gpsimd
        def _(pool):
            nc.gpsimd.memset(mhalf[:, :], -0.5).then_inc(s_half, 1)
            pool.sem_inc(s_gfree, OPEN)
            pool.wait_ge(s_half, 1)
            pool.wait_ge(s_bnvar, 1)
            nc.gpsimd.tensor_tensor(bn[:, 8:10], bn[:, 6:8], mhalf[:, :], ALU.pow).then_inc(s_bnrstd, 1)
            with pool.Fori(0, B) as b:
                pool.wait_ge(s_var, 2 * b + 1)
                nc.gpsimd.tensor_tensor(st[:, 6:7], st[:, 5:6], mhalf[:, 0:1], ALU.pow).then_inc(s_rstd, 1)
                pool.wait_ge(s_var, 2 * b + 2)
                nc.gpsimd.tensor_tensor(st[:, 25:26], st[:, 24:25], mhalf[:, 0:1], ALU.pow).then_inc(s_rstd, 1)
                for n in range(8):
                    pool.wait_ge(s_gw, OPEN + b * 8 + n + 1)
                    for odd in range(2):
                        for k in range(2):
                            for h in range(2):
                                kx = 2 * (2 * n + k) + odd
                                pool.dma_start(g_dram[bass.ds(b, 1), h, 2 * kx:2 * kx + 2].rearrange("b r c y -> (b c) r y"),
                                               g_st[n % 2][odd * C:(odd + 1) * C, k, :, h * HH:(h + 1) * HH])\
                                    .then_inc(s_gst[n % 2], 16)
                    if n:
                        pool.wait_ge(s_gst[(n - 1) % 2], (b * 4 + (n - 1) // 2 + 1) * G_DMAS * 16)
                        pool.sem_inc(s_gfree, 1)
                pool.wait_ge(s_gst[1], (b + 1) * 4 * G_DMAS * 16)
                pool.sem_inc(s_gfree, 1)

            def rows(b, u, j):
                pool.wait_ge(s_srow, OPEN + b * UNITS + u - 1)
                nc.gpsimd.tensor_copy(g_row[:, j % 2], g_all[:, :, bass.ds(u * UROW, UROW)].rearrange("p c y -> p y c"))\
                    .then_inc(s_grow, 1)

            with pool.Fori(0, B) as b:
                pool.wait_ge(s_gall, (b + 1) * 32)
                alone(pool)
                with pool.Fori(0, BODIES) as r:
                    for j in range(BODY):
                        rows(b, r * BODY + j, j)

        @block.vector
        def _(dve):
            v = nc.vector
            stt, ts, tt_ = v.scalar_tensor_tensor, v.tensor_scalar, v.tensor_tensor
            MUL, ADD, SUB = ALU.mult, ALU.add, ALU.subtract

            def chained(semaphore, base):
                count = [0]

                def link(ins):
                    count[0] += 1
                    ins.then_inc(semaphore, 1)
                    dve.wait_ge(semaphore, base + count[0])
                return link, count

            dve.sem_inc(s_reduced, OPEN)

            dve.sem_inc(s_spec, OPEN)
            dve.sem_inc(s_h, OPEN)
            dve.sem_inc(s_sacc, OPEN)
            dve.sem_inc(s_eacc, OPEN)

            dve.wait_ge(s_const, CONSTS)

            link, _n = chained(s_setup, 0)
            link(v.memset(ones[:, :], 1.0))
            for w in ("w1", "w2"):
                q = par[w][C:P, 0:C]
                link(ts(q, q, -1.0, None, MUL))
            link(ts(bn[:, 6:7], col(BN1RV), EPS, None, ADD))
            link(ts(bn[:, 7:8], col(BN2RV), EPS, None, ADD))
            v.tensor_copy(bn[:, 10:11], bn[:, 6:7]).then_inc(s_bnvar, 1)
            dve.wait_ge(s_bnrstd, 1)
            link(tt_(bn[:, 0:1], bn[:, 8:9], col(BN1G), MUL))
            link(tt_(bn[:, 1:2], col(G1B), col(BN1RM), SUB))
            link(stt(bn[:, 1:2], bn[:, 1:2], bn[:, 0:1], col(BN1B), MUL, ADD))
            link(ts(bn[:, 2:3], bn[:, 0:1], 1.0 / NPIX, None, MUL))
            link(tt_(bn[:, 4:5], bn[:, 9:10], col(BN2G), MUL))
            link(tt_(bn[:, 5:6], col(G2B), col(BN2RM), SUB))
            link(stt(bn[:, 5:6], bn[:, 5:6], bn[:, 4:5], col(BN2B), MUL, ADD))
            ts(bn[:, 3:4], col(CAB2), 2.0, None, MUL).then_inc(s_ready, 1)

            def s_(n):
                return st[:, n:n + 1]

            MEAN, MEANSQ = float(H) / (GC * NPIX), 1.0 / (GC * NPIX)
            with dve.Fori(0, B) as b:
                link, n_chain = chained(s_chain, b * CHAIN)
                for q in range(NG):
                    dve.wait_ge(s_square, OPEN + b * NG + q + 1)
                    v.tensor_reduce(sq_cg[:, :, q * CG:(q + 1) * CG], sq, AX.X, ADD).then_inc(s_reduced, 1)
                dve.wait_ge(s_reduced, OPEN + (b + 1) * NG)
                tt_(sq_dup[:, 0, :], sq_cg[:, 0, :], sq_cg[:, 1, :], ADD)
                tt_(sq_dup[:, 1, :], sq_cg[:, 0, :], sq_cg[:, 1, :], ADD).then_inc(s_stat, 1)
                dve.wait_ge(s_x, b + 1)
                link(v.tensor_copy(x_modes.rearrange("p (a n) -> p a n", a=2), ps[:, 4:6, :]))
                dve.wait_ge(s_sums, 3 * b + 1)
                link(v.tensor_copy(s_(0), ps[:, 6, 0:1]))
                v.tensor_copy(s_(1), x_modes[:, 0:1]).then_inc(s_stat, 1)
                dve.wait_ge(s_sums, 3 * b + 2)
                link(ts(s_(2), ps[:, 6, 3:4], MEAN, None, MUL))
                link(ts(s_(3), ps[:, 6, 2:3], MEANSQ, None, MUL))
                link(stt(s_(4), s_(2), s_(2), s_(3), MUL, SUB))
                ts(s_(5), s_(4), -1.0, EPS, MUL, ADD).then_inc(s_var, 1)
                dve.wait_ge(s_rstd, 2 * b + 1)
                link(tt_(s_(7), s_(6), col(GN1W), MUL))
                link(ts(s_(8), s_(7), 1.0, None, ADD))
                link(v.tensor_copy(alpha[:, bass.ds(b, 1)], s_(8)))
                link(stt(s_(9), s_(2), s_(7), col(GN1B), MUL, SUB))
                link(ts(h_modes, x_modes, s_(7), None, MUL))
                stt(h_modes[0:C, 0:1], st[0:C, 9:10], -float(H), h_modes[0:C, 0:1], MUL, ADD).then_inc(s_hm, 1)
                dve.wait_ge(s_w2, b + 1)
                link(ts(s_modes.rearrange("p (a n) -> p a n", a=2), ps[:, 6:8, :], col(AB2), None, ADD))
                stt(s_modes[0:C, 0:1], st[0:C, 9:10], -float(H), s_modes[0:C, 0:1], MUL, ADD).then_inc(s_s, 1)
                dve.wait_ge(s_s, b + 1)
                link(tt_(tmp1, s_modes, wgt_s, MUL))
                link(v.tensor_tensor_reduce(out=tmp1, in0=tmp1, in1=s_modes, scale=1.0, scalar=0.0, op0=MUL, op1=ADD,
                                            accum_out=s_(10)))
                link(tt_(tmp1, s_modes, wgt_x, MUL))
                link(v.tensor_tensor_reduce(out=tmp1, in0=tmp1, in1=x_modes, scale=1.0, scalar=0.0, op0=MUL, op1=ADD,
                                            accum_out=s_(11)))
                top = con["top"][:, 0:1]
                link(ts(s_(12), s_(0), s_(8), top, MUL, MUL))
                link(stt(s_(13), s_(11), 2.0, s_(12), MUL, ADD))
                link(stt(s_(16), s_(13), s_(8), s_(10), MUL, ADD))
                link(stt(s_(14), x_modes[:, 0:1], s_(8), s_modes[:, 0:1], MUL, ADD))
                tt_(s_(17), s_(14), top, MUL).then_inc(s_stat, 1)
                dve.wait_ge(s_sums, 3 * b + 3)
                link(ts(s_(21), ps[:, 6, 1:2], MEAN, None, MUL))
                link(ts(s_(22), ps[:, 6, 0:1], MEANSQ, None, MUL))
                link(stt(s_(23), s_(21), s_(21), s_(22), MUL, SUB))
                ts(s_(24), s_(23), -1.0, EPS, MUL, ADD).then_inc(s_var, 1)
                dve.wait_ge(s_rstd, 2 * b + 2)
                link(tt_(s_(26), s_(25), col(GN2W), MUL))
                stt(s_(20), s_(21), s_(26), col(GN2B), MUL, SUB).then_inc(s_nb2, 1)
                link(ts(fe_all[:, bass.ds(b, 1), :].rearrange("p a n -> p (a n)"), par["fe"][:, :], s_(26), None, MUL))
                dve.wait_ge(s_fs, b + 1)
                stt(febias[:, bass.ds(b, 1)], ps[:, 6, 4:5], -1.0, col(FEB), MUL, ADD).then_inc(s_spec, 1)
                dve.wait_ge(s_spec, OPEN + b + 1)
                assert n_chain[0] == CHAIN, n_chain

            def h_unit(b, u, l, s):
                dve.wait_ge(s_xl[s], (b * BODIES + l + 1) * 32)
                dve.wait_ge(s_srow, OPEN + b * UNITS + u + 1)
                hv = big_h[:, bass.ds(u * UPIX, UPIX)].rearrange("p (a n) -> p a n", a=2)
                stt(hv, hv, gt[:, 11:12], ps[:, 0:2, 0:2 * W], MUL, ADD).then_inc(s_h, 1)

            def shared_add(b, u):
                hv = big_h[:, bass.ds(u * UPIX, UPIX)]
                for k in range(2):
                    dve.wait_ge(s_shy, OPEN + (b * UNITS + u) * 2 + k + 1)
                    dve.wait_ge(s_sacc, OPEN + (b * UNITS + u) * 2 + k)
                    stt(hv, y_buf[:, k, 0:UPIX], 0.5, hv, MUL, ADD).then_inc(s_sacc, 1)

            def expert_add(b, p):
                hv = big_h[:, bass.ds(p * PAIR, PAIR)]
                for k in range(TOPK):
                    dve.wait_ge(s_exy, OPEN + (b * PAIRS + p) * TOPK + k + 1)
                    dve.wait_ge(s_eacc, OPEN + (b * PAIRS + p) * TOPK + k)
                    stt(hv, y_buf[:, k % 2, :], gate[:, k:k + 1], hv, MUL, ADD).then_inc(s_eacc, 1)

            with dve.Fori(0, B) as b:
                v.tensor_copy(fe_b[:, :], fe_all[:, bass.ds(b, 1), :].rearrange("p a n -> p (a n)"))
                v.tensor_copy(gt[:, 10:11], febias[:, bass.ds(b, 1)])
                link, n_chain = chained(s_gchain, b * GATE_CHAIN)
                link(v.tensor_copy(gt[:, 11:12], alpha[:, bass.ds(b, 1)]))
                v.tensor_copy(gt[:, 12:13], gt[:, 11:12]).then_inc(s_par, 1)
                for j in range(BODY):
                    h_unit(b, j, 0, j // 2)
                    if j:
                        shared_add(b, j - 1)
                with dve.Fori(1, BODIES) as r:
                    for j in range(BODY):
                        h_unit(b, r * BODY + j, r, j // 2)
                        shared_add(b, r * BODY + j - 1)
                shared_add(b, UNITS - 1)
                dve.wait_ge(s_feat, OPEN + (b + 1) * UNITS)
                v.tensor_reduce(gt[:, 0:1], gf_parts[:, :], AX.X, ADD).then_inc(s_gd, 1)
                dve.wait_ge(s_ga, 5 * b + 3)
                tt_(gt[:, 4:5], gt[:, 1:2], gt[:, 3:4], MUL).then_inc(s_gd, 1)
                dve.wait_ge(s_mm, 5 * b + 5)
                link(tt_(sc[:, :], ps[:, 0, 8:8 + E], par["g3b"][:, :], ADD))
                s_j = sc[:, :].rearrange("p (a j) -> p a j", a=1).to_broadcast([P, E, E])
                s_e = sc[:, :].rearrange("p (e a) -> p e a", a=1).to_broadcast([P, E, E])
                link(tt_(cmp_a[:, :, :], s_j, s_e, ALU.is_gt))
                link(tt_(cmp_b[:, :, :], s_j, s_e, ALU.is_equal))
                link(tt_(cmp_b[:, :, :], cmp_b[:, :, :], con["before"][:, :].rearrange("p (e j) -> p e j", e=E), MUL))
                link(tt_(cmp_a[:, :, :], cmp_a[:, :, :], cmp_b[:, :, :], ADD))
                link(v.tensor_reduce(rank[:, :], cmp_a[:, :, :], AX.X, ADD))
                over_k = lambda t: t.rearrange("p (a e) -> p a e", a=1).to_broadcast([P, TOPK, E])
                link(tt_(pick[:, :, :], con["slot"][:, :].rearrange("p (k e) -> p k e", k=TOPK), over_k(rank[:, :]),
                         ALU.is_equal))
                link(tt_(picked[:, :, :], pick[:, :, :], over_k(con["index"][:, :]), MUL))
                link(v.tensor_reduce(idxf[:, :], picked[:, :, :], AX.X, ADD))
                ts(idx[:, :], idxf[:, :], float(E - 1), None, ALU.min).then_inc(s_idx, 1)
                link(tt_(picked[:, :, :], pick[:, :, :], over_k(sc[:, :]), MUL))
                link(v.tensor_reduce(val[:, :], picked[:, :, :], AX.X, ADD))
                ts(gt[:, 6:7], val[:, 0:1], -1.0 / TEMPERATURE, None, MUL).then_inc(s_top, 1)
                dve.wait_ge(s_exp, b + 1)
                link(v.reciprocal(gt[:, 8:9], gt[:, 7:8]))
                link(ts(gate[:, :], ex[:, :], gt[:, 8:9], None, MUL))
                assert n_chain[0] == GATE_CHAIN, n_chain
                alone(dve)
                with dve.Fori(0, STEPS) as n:
                    for j in range(2):
                        expert_add(b, n * 2 + j)


def kernel(**inputs):
    import concourse.bacc as bacc
    from concourse.bass_utils import run_bass_kernel_spmd

    nc = bacc.Bacc("TRN2", target_bir_lowering=False, num_devices=1)
    arrays = {k: np.ascontiguousarray(a) for k, a in {**laid_out(inputs), **constants()}.items()}
    d = {k: nc.dram_tensor(k, a.shape, mybir.dt.from_np(a.dtype), kind="ExternalInput").ap() for k, a in arrays.items()}
    out = nc.dram_tensor("out", (B, C, H, W), F32, kind="ExternalOutput").ap()
    build(nc, d, out)
    r = run_bass_kernel_spmd(nc, [arrays], core_ids=[0])
    return r.results[0]["out"]
```

```python
from contextlib import ExitStack

import numpy as np

import concourse.bass as bass
from concourse import mybir

F32 = mybir.dt.float32
I32 = mybir.dt.int32
ALU = mybir.AluOpType
ACT = mybir.ActivationFunctionType
AX = mybir.AxisListType

B, C, H, W = 8, 64, 192, 192
MODES = 32
NB = 4
BS = C // NB
E, TOPK = 16, 4
GROUPS = 8
GC = C // GROUPS
NPIX = H * W
EPS = 1e-5
P = 128
HH = H // 2
HW2 = HH * W
NM = MODES * MODES
KR = 2 * MODES

CG = 8
NG = C // CG
XT = 2 * CG * W
SLOTS = 4

UROW = 4
UPIX = UROW * W
UNITS = HH // UROW
BODY = 4
BODIES = UNITS // BODY
LROW = 2 * UROW
LPIX = LROW * W
BANK = 512
PAIR = 2 * BANK
STEP = 2 * PAIR
STEPS = HW2 // STEP
PAIRS = 2 * STEPS

OPEN = 16
TEMPERATURE = 2.0
CQ = CG // 2
LAG = 2 * BODY
CHAIN, GATE_CHAIN = 24, 14


def constants():
    k = np.arange(MODES)
    n = np.arange(H)
    ang = 2 * np.pi * np.outer(n, k) / H
    cos, sin = np.cos(ang), np.sin(ang)
    by = np.stack([cos, -sin], axis=-1).reshape(2, HH, KR).transpose(1, 0, 2)
    bx = (np.stack([cos, sin], axis=1) / H).reshape(2, HH, KR).transpose(1, 0, 2)
    iy = np.zeros((2, MODES, 2, H))
    iy[0, :, 0], iy[1, :, 0] = cos.T, -sin.T
    iy[0, :, 1], iy[1, :, 1] = sin.T, cos.T
    iy = np.tile(iy.reshape(KR, 2 * H), (2, 1))
    twice = np.where(k == 0, 1.0, 2.0)[:, None] / H
    ix = np.stack([cos.T * twice, -sin.T * twice], axis=1)
    ix = np.concatenate([ix[0::2], ix[1::2]]).reshape(KR, W)
    ix = np.tile(ix, (2, 1))
    ws = np.full((2, MODES, MODES), 2.0)
    ws[:, :, 0] = 0.5
    ws[0, 0, 0], ws[1, 0, 0] = 1.0, 0.0
    wx = np.full((2, MODES, MODES), 2.0)
    wx[:, :, 0] = 1.0
    wx[1, 0, 0] = 0.0
    ws = np.repeat(ws.reshape(2, NM), C, axis=0)
    wx = np.repeat(wx.reshape(2, NM), C, axis=0)
    c = np.arange(P)
    same = ((c[:, None] % C) // GC == (c[None, :] % C) // GC)
    grp_top = same * (c[:, None] < C)
    eye = np.eye(P)
    turn = np.zeros((P, P))
    turn[C + np.arange(C), np.arange(C)] = 1.0
    turn[np.arange(C), C + np.arange(C)] = -1.0
    top = (c < C)[:, None]
    e = np.arange(E)
    before = np.tile((e[None, :] < e[:, None]).reshape(1, E * E), (P, 1))
    slot = np.tile(np.repeat(np.arange(TOPK), E)[None, :], (P, 1))
    index = np.tile(e[None, :], (P, 1))
    named = dict(by=by.reshape(HH, 2 * KR), bx=bx.reshape(HH, 2 * KR), iy=iy, ix=ix, ws=ws, wx=wx,
                 grp_top=grp_top, grp_all=same, eye=eye, turn=turn, top=top, before=before, slot=slot,
                 index=index)
    return {"k_" + n: np.ascontiguousarray(a, dtype=np.float32) for n, a in named.items()}


def block_diagonal(a):
    n, m = a.shape
    out = np.zeros((2 * n, 2 * m), a.dtype)
    out[:n, :m] = a
    out[n:, m:] = a
    return out


def laid_out(i):
    g = {k.removeprefix("L0_conv_"): np.asarray(v) for k, v in i.items()}

    def twice(v):
        return np.tile(v.reshape(-1, 1), (2, 1))

    def afno(w):
        full = np.zeros((2, C, 2, C), w.dtype)
        for n in range(NB):
            s = slice(n * BS, (n + 1) * BS)
            full[0, s, 0, s] = w[0, n]
            full[0, s, 1, s] = w[1, n]
            full[1, s, 0, s] = w[1, n]
            full[1, s, 1, s] = w[0, n]
        return full.reshape(P, P)

    experts = np.zeros((E, P, P + 1), g["expert_w"].dtype)
    for e in range(E):
        experts[e, :, :P] = block_diagonal(g["expert_w"][e].T)
        experts[e, :, P] = np.tile(g["expert_b"][e], 2)
    cols = [twice(g[n]) for n in ("gn1_w", "gn1_b", "gn2_w", "gn2_b", "fe_b")]
    cols += [twice(g["shared_b"][s]) for s in range(2)]
    cols += [g["afno_b1"].reshape(P, 1), g["afno_b2"].reshape(P, 1)]
    cols += [g[n].reshape(P, 1) for n in ("g1_b", "bn1_g", "bn1_b", "bn1_rm", "bn1_rv", "ca_b2")]
    pad = lambda v: np.concatenate([v.reshape(-1, 1), np.ones((P - v.size, 1), v.dtype)])
    cols += [pad(g[n]) for n in ("ca_b1", "g2_b", "bn2_g", "bn2_b", "bn2_rm", "bn2_rv")]
    return dict(
        x=g["x"],
        p_cols=np.concatenate(cols, axis=1),
        p_fe=block_diagonal(g["fe_w"].T), p_sh0=block_diagonal(g["shared_w"][0].T),
        p_sh1=block_diagonal(g["shared_w"][1].T), p_w1=afno(g["afno_w1"]), p_w2=afno(g["afno_w2"]),
        p_g1=np.tile(g["g1_w"].T, (2, 1)), p_ca1=g["ca_w1"].T, p_ca2=g["ca_w2"].T, p_g2=g["g2_w"].T,
        p_g3=g["g3_w"].T, p_g3b=np.tile(g["g3_b"].reshape(1, E), (P, 1)), p_experts=experts,
    )


(GN1W, GN1B, GN2W, GN2B, FEB, SB0, SB1, AB1, AB2, G1B, BN1G, BN1B, BN1RM, BN1RV, CAB2,
 CAB1, G2B, BN2G, BN2B, BN2RM, BN2RV) = range(21)


def build(nc, d, out):
    ctx = ExitStack()
    with ctx:
        def sb(name, shape, dt=F32):
            return ctx.enter_context(nc.sbuf_tensor(name, shape, dt))

        def sem(name):
            return ctx.enter_context(nc.semaphore(name))

        g_dram = nc.dram_tensor("g_scratch", [B, 2, KR, C, HH], F32, kind="Internal").ap()

        big_h = sb("big_h", [P, HW2])
        big_f = sb("big_f", [P, HW2])
        g_all = sb("g_all", [P, C, HH])
        g_row = sb("g_row", [P, 2, UROW, C])
        y_buf = sb("y_buf", [P, 2, PAIR])
        con = {}
        for name, width in (("by", 2 * KR), ("bx", 2 * KR), ("iy", 2 * H), ("ix", W), ("grp_top", P), ("grp_all", P),
                            ("eye", P), ("turn", P), ("top", 1), ("before", E * E), ("slot", TOPK * E),
                            ("index", E)):
            con[name] = sb("c_" + name, [HH if name in ("by", "bx") else P, width])
        par = {}
        for name, rows, width in (("cols", P, 21), ("fe", P, P), ("sh0", P, P), ("sh1", P, P), ("w1", P, P), ("w2", P, P),
                                  ("g1", P, P), ("ca1", P, E // 2), ("ca2", E // 2, P), ("g2", P, C), ("g3", C, E), ("g3b", P, E)):
            par[name] = sb("w_" + name, [rows, width])
        fe_all = sb("fe_all", [P, B, P])
        fe_b = sb("fe_b", [P, P])
        febias = sb("febias", [P, B])
        alpha = sb("alpha", [P, B])
        w_sel = sb("w_sel", [P, TOPK, P + 1])
        ones = sb("ones", [P, 1])
        mhalf = sb("mhalf", [P, 2])
        sq_cg = sb("sq_cg", [HH, 2, C])
        sq_dup = sb("sq_dup", [HH, 2, C])
        st = sb("st", [P, 32])
        bn = sb("bn", [P, 12])
        gf_parts = sb("gf_parts", [P, UNITS])
        gt = sb("gt", [P, 16])
        h2_wide = sb("h2_wide", [C, P])
        sc = sb("sc", [P, E])
        cmp_a = sb("cmp_a", [P, E, E])
        cmp_b = sb("cmp_b", [P, E, E])
        rank = sb("rank", [P, E])
        pick = sb("pick", [P, TOPK, E])
        picked = sb("picked", [P, TOPK, E])
        val = sb("val", [P, TOPK])
        ex = sb("ex", [P, TOPK])
        gate = sb("gate", [P, TOPK])
        idxf = sb("idxf", [P, TOPK])
        idx = sb("idx", [P, TOPK], I32)

        ps = ctx.enter_context(nc.psum_tensor("ps", [P, 8, BANK], F32))

        xt = [big_h[0:HH, s * XT:(s + 1) * XT].rearrange("p (h c x) -> p h c x", h=2, c=CG) for s in range(SLOTS)]
        sq = [big_h[0:HH, (SLOTS + n) * XT:(SLOTS + n + 1) * XT].rearrange("p (h c x) -> p h c x", h=2, c=CG) for n in range(2)]
        g_st = g_all[:, :, :].rearrange("p c y -> p (c y)").rearrange("p (n r y) -> p n r y", r=2, y=H)
        tt = big_f[0:HH, 0:2 * KR * C].rearrange("p (h k c) -> p h k c", h=2, k=KR)
        o = 2 * KR * C
        p_modes = big_f[:, o:o + 2 * NM].rearrange("p (k t q) -> p k t q", k=MODES, t=2)
        x_modes, h_modes, o1, s_modes, tmp1, st_modes = (big_f[:, o + n * NM:o + (n + 1) * NM] for n in range(2, 8))
        t_sb = [big_f[:, o + (8 + n) * NM:o + (8 + n) * NM + CQ * W].rearrange("p (c x) -> p c x", x=W) for n in range(2)]
        wgt_s, wgt_x = y_buf[:, 0, :], y_buf[:, 1, :]
        st_v = st_modes.rearrange("p (k c) -> p k c", c=C)

        s_const = sem("const_loaded")
        s_setup, s_bnvar, s_bnrstd = sem("setup_chain"), sem("bn_var_ready"), sem("bn_rstd_ready")
        s_ready, s_half = sem("setup_done"), sem("exponent_ready")
        s_passed, s_gfree = sem("wait_passed"), sem("g_staging_free")
        s_xt = [sem(f"xt_loaded{s}") for s in range(SLOTS)]
        s_gst = sem("g_stored")
        s_f1, s_t, s_tr, s_tt = sem("f1_done"), sem("t_written"), sem("t_turned"), sem("turned_written")
        s_square = sem("squared")
        s_f2, s_pm, s_x = sem("f2_done"), sem("p_written"), sem("x_done")
        s_stat, s_sums, s_var, s_rstd = sem("stats_ready"), sem("sums_done"), sem("variance_ready"), sem("rstd_ready")
        s_hm, s_w1, s_o1, s_w2, s_s = sem("h_modes_ready"), sem("w1_done"), sem("o1_written"), sem("w2_done"), sem("s_written")
        s_st, s_stw, s_g, s_gw = sem("st_done"), sem("st_written"), sem("g_done"), sem("g_written")
        s_nb2, s_fs, s_spec, s_chain = sem("shift2_ready"), sem("fe_shift_done"), sem("batch_modes_done"), sem("dve_chain")
        s_xl = [sem(f"x_loaded{s}") for s in range(2)]
        s_gall, s_grow, s_par = sem("g_loaded"), sem("g_rows_written"), sem("batch_weights_ready")
        s_srow, s_h, s_fe, s_feat = sem("s_rows_done"), sem("h_written"), sem("fe_done"), sem("feats_written")
        s_sh, s_shy, s_sacc = sem("shared_done"), sem("shared_gelu_done"), sem("shared_added")
        s_mm, s_ga, s_gd, s_exp = sem("gate_matmul_done"), sem("gate_act_done"), sem("gate_dve_done"), sem("gate_exp_done")
        s_gchain, s_top, s_idx, s_wsel = sem("gate_chain"), sem("gate_max_ready"), sem("indices_ready"), sem("experts_loaded")
        s_ex, s_exy, s_eacc, s_store = sem("expert_done"), sem("expert_gelu_done"), sem("expert_added"), sem("out_stored")
        block = ctx.enter_context(nc.Block())

        x_y = d["x"].rearrange("b (g c) (h y) w -> (b g) h y c w", g=NG, h=2)
        x_c = d["x"].rearrange("b c (h y) w -> b h c (y w)", h=2)
        out_c = out.rearrange("b c (h y) w -> b h c (y w)", h=2)
        CONSTS = (len(con) + len(par) + 2) * 16
        col = lambda n: par["cols"][:, n:n + 1]

        def alone(eng):
            eng.sem_inc(s_passed, 1)

        @block.sync
        def _(sp):
            sp.sem_inc(s_store, 16 * OPEN)
            for name, t in con.items():
                sp.dma_start(t[:, :], d["k_" + name]).then_inc(s_const, 16)
            for name, t in par.items():
                sp.dma_start(t[:, :], d["p_" + name]).then_inc(s_const, 16)
            sp.dma_start(wgt_s, d["k_ws"]).then_inc(s_const, 16)
            sp.dma_start(wgt_x, d["k_wx"]).then_inc(s_const, 16)

            with sp.Fori(0, B * NG // SLOTS) as r:
                for s in range(SLOTS):
                    sp.wait_ge(s_f1, OPEN + r * SLOTS + s - SLOTS + 1)
                    alone(sp)
                    sp.wait_ge(s_square, OPEN + r * SLOTS + s - SLOTS + 1)
                    alone(sp)
                    for h in range(2):
                        sp.dma_start(xt[s][:, h], x_y[bass.ds(r * SLOTS + s, 1), h].rearrange("q y c w -> (q y) c w"))\
                          .then_inc(s_xt[s], 16)

            sp.wait_ge(s_spec, OPEN + B)
            sp.wait_ge(s_gst, B * 8 * 16)

            def load_x(b, l, s):
                for h in range(2):
                    sp.dma_start(big_h[h * C:(h + 1) * C, bass.ds(l * LPIX, LPIX)],
                                 x_c[bass.ds(b, 1), h, :, bass.ds(l * LPIX, LPIX)].rearrange("b c n -> (b c) n"))\
                      .then_inc(s_xl[s], 16)

            def load_g(b):
                for h in range(2):
                    sp.dma_start(g_all[h * KR:(h + 1) * KR], g_dram[bass.ds(b, 1), h].rearrange("b m c y -> (b m) c y"))\
                      .then_inc(s_gall, 16)

            def store(b, n):
                sp.wait_ge(s_eacc, OPEN + (b * PAIRS + (n + 1) * 2) * TOPK)
                alone(sp)
                sp.wait_ge(s_store, 16 * OPEN + (b * STEPS + n) * 32)
                alone(sp)
                for h in range(2):
                    sp.dma_start(out_c[bass.ds(b, 1), h, :, bass.ds(n * STEP, STEP)].rearrange("b c n -> (b c) n"),
                                 big_h[h * C:(h + 1) * C, bass.ds(n * STEP, STEP)]).then_inc(s_store, 16)

            def batch(b, last):
                with sp.Fori(1, BODIES) as r:
                    for l in range(2):
                        sp.wait_ge(s_h, OPEN + b * UNITS + (r - 1) * BODY + 2 * l + 2)
                        alone(sp)
                        load_x(b, r * 2 + l, l)
                sp.wait_ge(s_idx, b + 1)
                alone(sp)
                for k in range(TOPK):
                    e = sp.value_load(idx[0:1, k:k + 1], min_val=0, max_val=E - 1)
                    sp.dma_start(w_sel[:, k], d["p_experts"][bass.ds(e, 1)].rearrange("e p n -> (e p) n")).then_inc(s_wsel, 16)
                for n in range(2):
                    store(b, n)
                if not last:
                    sp.wait_ge(s_grow, (b + 1) * UNITS)
                    alone(sp)
                    load_g(b + 1)
                    sp.wait_ge(s_store, 16 * OPEN + (b * STEPS + 2) * 32)
                    alone(sp)
                    for l in range(2):
                        load_x(b + 1, l, l)
                with sp.Fori(2, STEPS) as n:
                    store(b, n)
                sp.wait_ge(s_store, 16 * OPEN + (b + 1) * STEPS * 32)
                alone(sp)

            load_g(0)
            for l in range(2):
                load_x(0, l, l)
            with sp.Fori(0, B - 1) as b:
                batch(b, False)
            batch(B - 1, True)

        @block.tensor
        def _(pe):
            mm = nc.tensor.matmul
            pe.wait_ge(s_const, CONSTS)
            pe.wait_ge(s_ready, 1)
            pe.sem_inc(s_f1, OPEN)
            pe.sem_inc(s_f2, OPEN)
            pe.sem_inc(s_tr, OPEN)
            pe.sem_inc(s_srow, OPEN)

            def f1(b, q):
                s = q % SLOTS
                pe.wait_ge(s_xt[s], (b * 2 + q // SLOTS + 1) * 32)
                pe.wait_ge(s_t, OPEN + b * NG + q)
                alone(pe)
                for c2 in range(CQ // 2):
                    for h in range(2):
                        for cq in range(2):
                            c = cq * CQ + 2 * c2
                            i = mm(ps[cq * KR:(cq + 1) * KR, c2, 0:2 * W], con["by"][:, h * KR:(h + 1) * KR],
                                   xt[s][:, h, c:c + 2, :].rearrange("p c x -> p (c x)"), start=(h == 0), stop=(h == 1))
                i.then_inc(s_f1, 1)

            def turn(b, q):
                pe.wait_ge(s_t, OPEN + b * NG + q + 1)
                pe.wait_ge(s_tt, OPEN + b * NG + q)
                for xc in range(2):
                    for c in range(CQ):
                        i = nc.tensor.transpose(ps[0:HH, 2 + xc, c * P:(c + 1) * P], t_sb[q % 2][:, c, xc * HH:(xc + 1) * HH],
                                                con["eye"][:, :])
                i.then_inc(s_tr, 1)

            def modes(b, tiles):
                def tile(q):
                    if tiles and q < NG:
                        f1(b + 1, q)
                    if tiles and q >= 1:
                        turn(b + 1, q - 1)

                pe.wait_ge(s_tt, OPEN + (b + 1) * NG)
                pe.wait_ge(s_gw, OPEN + b * 8)
                for ky in range(MODES):
                    for xc in range(2):
                        i = mm(ps[:, 4 + ky // 8, (ky % 8) * KR:(ky % 8 + 1) * KR],
                               tt[:, xc, 2 * ky:2 * ky + 2, :].rearrange("p k c -> p (k c)"),
                               con["bx"][:, xc * KR:(xc + 1) * KR], start=(xc == 0), stop=(xc == 1))
                i.then_inc(s_f2, 1)
                tile(0)
                pe.wait_ge(s_pm, b + 1)
                for half in range(2):
                    k = slice(half * 16, half * 16 + 16)
                    mm(ps[:, 4 + half, :], con["eye"][:, :], p_modes[:, k, 0, :], start=True, stop=False)
                    i = mm(ps[:, 4 + half, :], con["turn"][:, :], p_modes[:, k, 1, :], start=False, stop=True)
                i.then_inc(s_x, 1)
                pe.wait_ge(s_stat, 3 * b + 1)
                mm(ps[:, 6, 0:1], sq_dup[:, :, :].rearrange("p a c -> p (a c)"), ones[0:HH, :], start=True, stop=True)\
                    .then_inc(s_sums, 1)
                tile(1)
                pe.wait_ge(s_stat, 3 * b + 2)
                mm(ps[:, 6, 2:4], con["grp_top"][:, :], st[:, 0:2], start=True, stop=True).then_inc(s_sums, 1)
                tile(2)
                pe.wait_ge(s_hm, b + 1)
                for half in range(2):
                    i = mm(ps[:, 4 + half, :], par["w1"][:, :], h_modes[:, half * BANK:(half + 1) * BANK], start=True, stop=True)
                i.then_inc(s_w1, 1)
                tile(3)
                pe.wait_ge(s_o1, b + 1)
                for half in range(2):
                    i = mm(ps[:, 6 + half, :], par["w2"][:, :], o1[:, half * BANK:(half + 1) * BANK], start=True, stop=True)
                i.then_inc(s_w2, 1)
                tile(4)
                pe.wait_ge(s_s, b + 1)
                alone(pe)
                s_k = s_modes.rearrange("p (ky kx) -> p kx ky", ky=MODES)
                for kx in range(MODES):
                    for ri in range(2):
                        p0 = (kx % 2) * KR + ri * MODES
                        n = kx // 2
                        rows = slice(ri * C, (ri + 1) * C)
                        i = mm(ps[p0:p0 + MODES, 4 + n // 8, (n % 8) * C:(n % 8 + 1) * C], s_k[rows, kx, :],
                               con["eye"][rows, rows], start=True, stop=True)
                i.then_inc(s_st, 1)
                tile(5)
                pe.wait_ge(s_stat, 3 * b + 3)
                mm(ps[:, 6, 0:2], con["grp_all"][:, :], st[:, 16:18], start=True, stop=True).then_inc(s_sums, 1)
                pe.wait_ge(s_stw, b + 1)
                alone(pe)
                for g in range(8):
                    if g == 1:
                        tile(6)
                        pe.wait_ge(s_nb2, b + 1)
                        mm(ps[:, 6, 4:5], par["fe"][:, :], st[:, 20:21], start=True, stop=True).then_inc(s_fs, 1)
                        tile(7)
                        pe.wait_ge(s_spec, OPEN + b + 1)
                        alone(pe)
                    if g >= 2:
                        pe.wait_ge(s_gw, OPEN + b * 8 + g - 1)
                        alone(pe)
                    for n in (2 * g, 2 * g + 1):
                        for odd in range(2):
                            r = slice(odd * KR, (odd + 1) * KR)
                            i = mm(ps[odd * C:(odd + 1) * C, 4 + n % 4, 0:2 * H], st_v[r, n, :], con["iy"][r, :],
                                   start=True, stop=True)
                    i.then_inc(s_g, 1)
                    if g == 1:
                        tile(8)

            for q in range(NG):
                f1(0, q)
                if q:
                    turn(0, q - 1)
            turn(0, NG - 1)
            with pe.Fori(0, B - 1) as b:
                modes(b, True)
            modes(B - 1, False)

            def srows(b, u, j):
                pe.wait_ge(s_grow, b * UNITS + u + 1)
                pe.wait_ge(s_h, OPEN + b * UNITS + u)
                alone(pe)
                for r in range(UROW):
                    for h in range(2):
                        k = slice(h * C, (h + 1) * C)
                        i = mm(ps[k, r // 2, (r % 2) * W:(r % 2 + 1) * W], g_row[k, j % 2, r, :], con["ix"][k, :],
                               start=True, stop=True)
                i.then_inc(s_srow, 1)

            def fe(b, u):
                pe.wait_ge(s_h, OPEN + b * UNITS + u + 1)
                pe.wait_ge(s_feat, OPEN + b * UNITS + u)
                for half in range(2):
                    i = mm(ps[:, 2 + half, 0:2 * W], fe_b[:, :], big_h[:, bass.ds(u * UPIX + half * 2 * W, 2 * W)],
                           start=True, stop=True)
                i.then_inc(s_fe, 1)

            def shared(b, u):
                pe.wait_ge(s_feat, OPEN + b * UNITS + u + 1)
                for k in range(2):
                    pe.wait_ge(s_shy, OPEN + (b * UNITS + u - 1) * 2 + k + 1)
                    for half in range(2):
                        i = mm(ps[:, 4 + 2 * k + half, 0:2 * W], par[f"sh{k}"][:, :],
                               big_f[:, bass.ds(u * UPIX + half * 2 * W, 2 * W)], start=True, stop=True)
                    i.then_inc(s_sh, 1)

            def expert(b, p):
                for k in range(TOPK):
                    pe.wait_ge(s_exy, OPEN + (b * PAIRS + p - 1) * TOPK + k + 1)
                    for half in range(2):
                        i = mm(ps[:, 2 * k + half, :], w_sel[:, k, 0:P], big_f[:, bass.ds(p * PAIR + half * BANK, BANK)],
                               start=True, stop=True)
                    i.then_inc(s_ex, 1)

            pe.wait_ge(s_gw, OPEN + B * 8)
            with pe.Fori(0, B) as b:
                pe.wait_ge(s_par, b + 1)
                pe.wait_ge(s_exy, OPEN + b * PAIRS * TOPK)
                for u in range(LAG):
                    srows(b, u, u)
                    if u:
                        fe(b, u - 1)
                with pe.Fori(LAG // BODY, BODIES) as r:
                    for j in range(BODY):
                        srows(b, r * BODY + j, j)
                        fe(b, r * BODY + j - 1)
                        shared(b, r * BODY + j - LAG)
                fe(b, UNITS - 1)
                shared(b, UNITS - 8)
                pe.wait_ge(s_gd, 2 * b + 1)
                mm(ps[:, 0, 0:1], par["g1"][:, :], gt[:, 0:1], start=True, stop=True).then_inc(s_mm, 1)
                shared(b, UNITS - 7)
                pe.wait_ge(s_ga, 5 * b + 1)
                mm(ps[0:E // 2, 0, 1:2], par["ca1"][:, :], gt[:, 1:2], start=True, stop=True).then_inc(s_mm, 1)
                shared(b, UNITS - 6)
                pe.wait_ge(s_ga, 5 * b + 2)
                mm(ps[:, 0, 2:3], par["ca2"][:, :], gt[0:E // 2, 2:3], start=True, stop=True).then_inc(s_mm, 1)
                shared(b, UNITS - 5)
                pe.wait_ge(s_gd, 2 * b + 2)
                mm(ps[0:C, 0, 3:4], par["g2"][:, :], gt[:, 4:5], start=True, stop=True).then_inc(s_mm, 1)
                shared(b, UNITS - 4)
                pe.wait_ge(s_ga, 5 * b + 5)
                mm(ps[:, 0, 8:8 + E], h2_wide[:, :], par["g3"][:, :], start=True, stop=True).then_inc(s_mm, 1)
                for u in range(UNITS - 3, UNITS):
                    shared(b, u)
                pe.wait_ge(s_wsel, (b + 1) * TOPK * 16)
                pe.wait_ge(s_shy, OPEN + (b + 1) * UNITS * 2)
                alone(pe)
                with pe.Fori(0, STEPS) as n:
                    for j in range(2):
                        expert(b, n * 2 + j)

        @block.scalar
        def _(act):
            a = nc.scalar.activation
            act.wait_ge(s_const, CONSTS)
            act.wait_ge(s_ready, 1)
            act.sem_inc(s_t, OPEN)
            act.sem_inc(s_tt, OPEN)
            act.sem_inc(s_gw, OPEN)
            act.sem_inc(s_feat, OPEN)
            act.sem_inc(s_shy, OPEN)
            act.sem_inc(s_exy, OPEN)

            def t_out(b, q):
                act.wait_ge(s_f1, OPEN + b * NG + q + 1)
                act.wait_ge(s_tr, OPEN + b * NG + q - 1)
                a(t_sb[q % 2].rearrange("p (a c) x -> p a (c x)", a=2), ps[:, 0:2, 0:2 * W], ACT.Copy).then_inc(s_t, 1)

            def turned_out(b, q):
                act.wait_ge(s_tr, OPEN + b * NG + q + 1)
                act.wait_ge(s_f2, OPEN + b)
                for xc in range(2):
                    src = ps[0:HH, 2 + xc, :].rearrange("p (c u k) -> p k u c", c=CQ, u=2)
                    dst = tt[:, xc, :, q * CG:(q + 1) * CG].rearrange("p k (u c) -> p k u c", u=2)
                    i = a(dst, src, ACT.Copy)
                i.then_inc(s_tt, 1)

            def modes(b, tiles):
                def tile(q):
                    if tiles and q < NG:
                        t_out(b + 1, q)
                    if tiles and q >= 1:
                        turned_out(b + 1, q - 1)

                act.wait_ge(s_f2, OPEN + b + 1)
                a(p_modes.rearrange("p k t q -> p (k t q)").rearrange("p (a n) -> p a n", a=4), ps[:, 4:8, :], ACT.Copy)\
                    .then_inc(s_pm, 1)
                for q in range(4):
                    tile(q)
                    if q == 2:
                        act.wait_ge(s_w1, b + 1)
                        a(o1.rearrange("p (a n) -> p a n", a=2), ps[:, 4:6, :], ACT.Gelu, bias=col(AB1)).then_inc(s_o1, 1)
                tile(4)
                act.wait_ge(s_st, b + 1)
                a(st_modes.rearrange("p (a n) -> p a n", a=2), ps[:, 4:6, :], ACT.Copy).then_inc(s_stw, 1)
                tile(5)
                act.wait_ge(s_gfree, OPEN + b)
                for g in range(8):
                    if g == 1:
                        tile(6)
                        tile(7)
                    act.wait_ge(s_g, b * 8 + g + 1)
                    bank = (4, 6)[g % 2]
                    a(g_st[:, 2 * g:2 * g + 2].rearrange("p n r y -> p n (r y)"), ps[:, bank:bank + 2, 0:2 * H], ACT.Copy)\
                        .then_inc(s_gw, 1)
                    if g == 1:
                        tile(8)

            for q in range(NG):
                t_out(0, q)
                if q:
                    turned_out(0, q - 1)
            turned_out(0, NG - 1)
            with act.Fori(0, B - 1) as b:
                modes(b, True)
            modes(B - 1, False)

            def feats(b, u):
                act.wait_ge(s_fe, b * UNITS + u + 1)
                a(big_f[:, bass.ds(u * UPIX, UPIX)].rearrange("p (a n) -> p a n", a=2), ps[:, 2:4, 0:2 * W], ACT.Gelu,
                  bias=gt[:, 10:11], accum_out=gf_parts[:, bass.ds(u, 1)]).then_inc(s_feat, 1)

            def shared_gelu(b, u):
                for k in range(2):
                    act.wait_ge(s_sh, (b * UNITS + u) * 2 + k + 1)
                    act.wait_ge(s_sacc, OPEN + (b * UNITS + u - 1) * 2 + k + 1)
                    a(y_buf[:, k, 0:UPIX].rearrange("p (a n) -> p a n", a=2), ps[:, 4 + 2 * k:6 + 2 * k, 0:2 * W], ACT.Gelu,
                      bias=col(SB0 + k)).then_inc(s_shy, 1)

            def expert_gelu(b, p):
                for k in range(TOPK):
                    act.wait_ge(s_ex, (b * PAIRS + p) * TOPK + k + 1)
                    act.wait_ge(s_eacc, OPEN + (b * PAIRS + p) * TOPK + k - 1)
                    a(y_buf[:, k % 2, :].rearrange("p (a n) -> p a n", a=2), ps[:, 2 * k:2 * k + 2, :], ACT.Gelu,
                      bias=w_sel[:, k, P:P + 1]).then_inc(s_exy, 1)

            act.wait_ge(s_spec, OPEN + B)
            with act.Fori(0, B) as b:
                act.wait_ge(s_par, b + 1)
                act.wait_ge(s_eacc, OPEN + b * PAIRS * TOPK)
                for u in range(LAG - 1):
                    feats(b, u)
                with act.Fori(LAG // BODY, BODIES) as r:
                    for j in range(BODY):
                        feats(b, r * BODY + j - 1)
                        shared_gelu(b, r * BODY + j - LAG)
                feats(b, UNITS - 1)
                shared_gelu(b, UNITS - 8)
                act.wait_ge(s_mm, 5 * b + 1)
                a(gt[:, 1:2], ps[:, 0, 0:1], ACT.Gelu, bias=bn[:, 1:2], scale=bn[:, 2:3]).then_inc(s_ga, 1)
                shared_gelu(b, UNITS - 7)
                act.wait_ge(s_mm, 5 * b + 2)
                a(gt[0:E // 2, 2:3], ps[0:E // 2, 0, 1:2], ACT.Gelu, bias=par["cols"][0:E // 2, CAB1:CAB1 + 1])\
                    .then_inc(s_ga, 1)
                shared_gelu(b, UNITS - 6)
                act.wait_ge(s_mm, 5 * b + 3)
                a(gt[:, 3:4], ps[:, 0, 2:3], ACT.Sigmoid, bias=bn[:, 3:4], scale=2.0).then_inc(s_ga, 1)
                shared_gelu(b, UNITS - 5)
                act.wait_ge(s_mm, 5 * b + 4)
                a(gt[0:C, 5:6], ps[0:C, 0, 3:4], ACT.Gelu, bias=bn[0:C, 5:6], scale=bn[0:C, 4:5]).then_inc(s_ga, 1)
                act.wait_ge(s_ga, 5 * b + 4)
                a(h2_wide[:, :], con["eye"][0:C, :], ACT.Identity, bias=gt[0:C, 5:6], scale=0.0).then_inc(s_ga, 1)
                shared_gelu(b, UNITS - 4)
                for u in range(UNITS - 3, UNITS):
                    shared_gelu(b, u)
                act.wait_ge(s_top, b + 1)
                a(ex[:, :], val[:, :], ACT.Exp, bias=gt[:, 6:7], scale=1.0 / TEMPERATURE, accum_out=gt[:, 7:8])\
                    .then_inc(s_exp, 1)
                act.wait_ge(s_wsel, (b + 1) * TOPK * 16)
                act.wait_ge(s_sacc, OPEN + (b + 1) * UNITS * 2)
                alone(act)
                with act.Fori(0, STEPS) as n:
                    for j in range(2):
                        expert_gelu(b, n * 2 + j)

        @block.gpsimd
        def _(pool):
            nc.gpsimd.memset(mhalf[:, :], -0.5).then_inc(s_half, 1)
            pool.sem_inc(s_gfree, OPEN)
            pool.wait_ge(s_half, 1)
            pool.wait_ge(s_bnvar, 1)
            nc.gpsimd.tensor_tensor(bn[:, 8:10], bn[:, 6:8], mhalf[:, :], ALU.pow).then_inc(s_bnrstd, 1)
            with pool.Fori(0, B) as b:
                pool.wait_ge(s_var, 2 * b + 1)
                nc.gpsimd.tensor_tensor(st[:, 6:7], st[:, 5:6], mhalf[:, 0:1], ALU.pow).then_inc(s_rstd, 1)
                pool.wait_ge(s_var, 2 * b + 2)
                nc.gpsimd.tensor_tensor(st[:, 25:26], st[:, 24:25], mhalf[:, 0:1], ALU.pow).then_inc(s_rstd, 1)
                for half in range(2):
                    n = slice(half * 8, half * 8 + 8)
                    pool.wait_ge(s_gw, OPEN + b * 8 + half * 4 + 4)
                    for odd in range(2):
                        for h in range(2):
                            m = odd * MODES + half * 16
                            pool.dma_start(g_dram[bass.ds(b, 1), h, m:m + 16].rearrange("b m c y -> (b c) m y"),
                                           g_st[odd * C:(odd + 1) * C, n, :, h * HH:(h + 1) * HH].rearrange("p n r y -> p (n r) y"))\
                                .then_inc(s_gst, 16)
                pool.wait_ge(s_gst, (b + 1) * 8 * 16)
                pool.sem_inc(s_gfree, 1)

            def rows(b, u, j):
                pool.wait_ge(s_srow, OPEN + b * UNITS + u - 1)
                nc.gpsimd.tensor_copy(g_row[:, j % 2], g_all[:, :, bass.ds(u * UROW, UROW)].rearrange("p c y -> p y c"))\
                    .then_inc(s_grow, 1)

            with pool.Fori(0, B) as b:
                pool.wait_ge(s_gall, (b + 1) * 32)
                alone(pool)
                with pool.Fori(0, BODIES) as r:
                    for j in range(BODY):
                        rows(b, r * BODY + j, j)

        @block.vector
        def _(dve):
            v = nc.vector
            stt, ts, tt_ = v.scalar_tensor_tensor, v.tensor_scalar, v.tensor_tensor
            MUL, ADD, SUB = ALU.mult, ALU.add, ALU.subtract

            def chained(semaphore, base):
                count = [0]

                def link(ins):
                    count[0] += 1
                    ins.then_inc(semaphore, 1)
                    dve.wait_ge(semaphore, base + count[0])
                return link, count

            dve.sem_inc(s_square, OPEN)

            dve.sem_inc(s_spec, OPEN)
            dve.sem_inc(s_h, OPEN)
            dve.sem_inc(s_sacc, OPEN)
            dve.sem_inc(s_eacc, OPEN)

            dve.wait_ge(s_const, CONSTS)

            link, _n = chained(s_setup, 0)
            link(v.memset(ones[:, :], 1.0))
            for w in ("w1", "w2"):
                q = par[w][C:P, 0:C]
                link(ts(q, q, -1.0, None, MUL))
            link(ts(bn[:, 6:7], col(BN1RV), EPS, None, ADD))
            link(ts(bn[:, 7:8], col(BN2RV), EPS, None, ADD))
            v.tensor_copy(bn[:, 10:11], bn[:, 6:7]).then_inc(s_bnvar, 1)
            dve.wait_ge(s_bnrstd, 1)
            link(tt_(bn[:, 0:1], bn[:, 8:9], col(BN1G), MUL))
            link(tt_(bn[:, 1:2], col(G1B), col(BN1RM), SUB))
            link(stt(bn[:, 1:2], bn[:, 1:2], bn[:, 0:1], col(BN1B), MUL, ADD))
            link(ts(bn[:, 2:3], bn[:, 0:1], 1.0 / NPIX, None, MUL))
            link(tt_(bn[:, 4:5], bn[:, 9:10], col(BN2G), MUL))
            link(tt_(bn[:, 5:6], col(G2B), col(BN2RM), SUB))
            link(stt(bn[:, 5:6], bn[:, 5:6], bn[:, 4:5], col(BN2B), MUL, ADD))
            ts(bn[:, 3:4], col(CAB2), 2.0, None, MUL).then_inc(s_ready, 1)

            def s_(n):
                return st[:, n:n + 1]

            MEAN, MEANSQ = float(H) / (GC * NPIX), 1.0 / (GC * NPIX)
            def squares(b, q):
                s = q % SLOTS
                dve.wait_ge(s_xt[s], (b * 2 + q // SLOTS + 1) * 32)
                dve.wait_ge(s_square, OPEN + b * NG + q - 1)
                for h in range(2):
                    for c in range(CG):
                        i = v.tensor_tensor_reduce(out=sq[q % 2][:, h, c, :], in0=xt[s][:, h, c, :], in1=xt[s][:, h, c, :], scale=1.0,
                                                   scalar=0.0, op0=MUL, op1=ADD, accum_out=sq_cg[:, h, q * CG + c:q * CG + c + 1])
                i.then_inc(s_square, 1)

            def modes(b, tiles):
                link, n_chain = chained(s_chain, b * CHAIN)

                def tile(q):
                    if tiles:
                        squares(b + 1, q)

                dve.wait_ge(s_square, OPEN + (b + 1) * NG)
                tt_(sq_dup[:, 0, :], sq_cg[:, 0, :], sq_cg[:, 1, :], ADD)
                tt_(sq_dup[:, 1, :], sq_cg[:, 0, :], sq_cg[:, 1, :], ADD).then_inc(s_stat, 1)
                dve.wait_ge(s_stat, 3 * b + 1)
                tile(0)
                tile(1)
                dve.wait_ge(s_x, b + 1)
                link(v.tensor_copy(x_modes.rearrange("p (a n) -> p a n", a=2), ps[:, 4:6, :]))
                dve.wait_ge(s_sums, 3 * b + 1)
                link(v.tensor_copy(s_(0), ps[:, 6, 0:1]))
                v.tensor_copy(s_(1), x_modes[:, 0:1]).then_inc(s_stat, 1)
                tile(2)
                dve.wait_ge(s_sums, 3 * b + 2)
                link(ts(s_(2), ps[:, 6, 3:4], MEAN, None, MUL))
                link(ts(s_(3), ps[:, 6, 2:3], MEANSQ, None, MUL))
                link(stt(s_(4), s_(2), s_(2), s_(3), MUL, SUB))
                ts(s_(5), s_(4), -1.0, EPS, MUL, ADD).then_inc(s_var, 1)
                dve.wait_ge(s_rstd, 2 * b + 1)
                link(tt_(s_(7), s_(6), col(GN1W), MUL))
                link(ts(s_(8), s_(7), 1.0, None, ADD))
                link(v.tensor_copy(alpha[:, bass.ds(b, 1)], s_(8)))
                link(stt(s_(9), s_(2), s_(7), col(GN1B), MUL, SUB))
                link(ts(h_modes, x_modes, s_(7), None, MUL))
                stt(h_modes[0:C, 0:1], st[0:C, 9:10], -float(H), h_modes[0:C, 0:1], MUL, ADD).then_inc(s_hm, 1)
                tile(3)
                dve.wait_ge(s_w2, b + 1)
                link(ts(s_modes.rearrange("p (a n) -> p a n", a=2), ps[:, 6:8, :], col(AB2), None, ADD))
                stt(s_modes[0:C, 0:1], st[0:C, 9:10], -float(H), s_modes[0:C, 0:1], MUL, ADD).then_inc(s_s, 1)
                dve.wait_ge(s_s, b + 1)
                tile(4)
                link(tt_(tmp1, s_modes, wgt_s, MUL))
                link(v.tensor_tensor_reduce(out=tmp1, in0=tmp1, in1=s_modes, scale=1.0, scalar=0.0, op0=MUL, op1=ADD,
                                            accum_out=s_(10)))
                link(tt_(tmp1, s_modes, wgt_x, MUL))
                link(v.tensor_tensor_reduce(out=tmp1, in0=tmp1, in1=x_modes, scale=1.0, scalar=0.0, op0=MUL, op1=ADD,
                                            accum_out=s_(11)))
                top = con["top"][:, 0:1]
                link(ts(s_(12), s_(0), s_(8), top, MUL, MUL))
                link(stt(s_(13), s_(11), 2.0, s_(12), MUL, ADD))
                link(stt(s_(16), s_(13), s_(8), s_(10), MUL, ADD))
                link(stt(s_(14), x_modes[:, 0:1], s_(8), s_modes[:, 0:1], MUL, ADD))
                tt_(s_(17), s_(14), top, MUL).then_inc(s_stat, 1)
                tile(5)
                dve.wait_ge(s_sums, 3 * b + 3)
                link(ts(s_(21), ps[:, 6, 1:2], MEAN, None, MUL))
                link(ts(s_(22), ps[:, 6, 0:1], MEANSQ, None, MUL))
                link(stt(s_(23), s_(21), s_(21), s_(22), MUL, SUB))
                ts(s_(24), s_(23), -1.0, EPS, MUL, ADD).then_inc(s_var, 1)
                dve.wait_ge(s_rstd, 2 * b + 2)
                link(tt_(s_(26), s_(25), col(GN2W), MUL))
                stt(s_(20), s_(21), s_(26), col(GN2B), MUL, SUB).then_inc(s_nb2, 1)
                link(ts(fe_all[:, bass.ds(b, 1), :].rearrange("p a n -> p (a n)"), par["fe"][:, :], s_(26), None, MUL))
                dve.wait_ge(s_fs, b + 1)
                stt(febias[:, bass.ds(b, 1)], ps[:, 6, 4:5], -1.0, col(FEB), MUL, ADD).then_inc(s_spec, 1)
                dve.wait_ge(s_spec, OPEN + b + 1)
                assert n_chain[0] == CHAIN, n_chain
                tile(6)
                tile(7)

            for q in range(NG):
                squares(0, q)
            with dve.Fori(0, B - 1) as b:
                modes(b, True)
            modes(B - 1, False)

            def h_unit(b, u, l, s):
                dve.wait_ge(s_xl[s], (b * BODIES + l + 1) * 32)
                dve.wait_ge(s_srow, OPEN + b * UNITS + u + 1)
                hv = big_h[:, bass.ds(u * UPIX, UPIX)].rearrange("p (a n) -> p a n", a=2)
                stt(hv, hv, gt[:, 11:12], ps[:, 0:2, 0:2 * W], MUL, ADD).then_inc(s_h, 1)

            def shared_add(b, u):
                hv = big_h[:, bass.ds(u * UPIX, UPIX)]
                for k in range(2):
                    dve.wait_ge(s_shy, OPEN + (b * UNITS + u) * 2 + k + 1)
                    dve.wait_ge(s_sacc, OPEN + (b * UNITS + u) * 2 + k)
                    stt(hv, y_buf[:, k, 0:UPIX], 0.5, hv, MUL, ADD).then_inc(s_sacc, 1)

            def expert_add(b, p):
                hv = big_h[:, bass.ds(p * PAIR, PAIR)]
                for k in range(TOPK):
                    dve.wait_ge(s_exy, OPEN + (b * PAIRS + p) * TOPK + k + 1)
                    dve.wait_ge(s_eacc, OPEN + (b * PAIRS + p) * TOPK + k)
                    stt(hv, y_buf[:, k % 2, :], gate[:, k:k + 1], hv, MUL, ADD).then_inc(s_eacc, 1)

            with dve.Fori(0, B) as b:
                v.tensor_copy(fe_b[:, :], fe_all[:, bass.ds(b, 1), :].rearrange("p a n -> p (a n)"))
                v.tensor_copy(gt[:, 10:11], febias[:, bass.ds(b, 1)])
                link, n_chain = chained(s_gchain, b * GATE_CHAIN)
                link(v.tensor_copy(gt[:, 11:12], alpha[:, bass.ds(b, 1)]))
                v.tensor_copy(gt[:, 12:13], gt[:, 11:12]).then_inc(s_par, 1)
                for u in range(LAG):
                    h_unit(b, u, u // BODY, u % BODY // 2)
                with dve.Fori(LAG // BODY, BODIES) as r:
                    for j in range(BODY):
                        h_unit(b, r * BODY + j, r, j // 2)
                        shared_add(b, r * BODY + j - LAG)
                dve.wait_ge(s_feat, OPEN + (b + 1) * UNITS)
                v.tensor_reduce(gt[:, 0:1], gf_parts[:, :], AX.X, ADD).then_inc(s_gd, 1)
                for u in range(UNITS - 8, UNITS - 5):
                    shared_add(b, u)
                dve.wait_ge(s_ga, 5 * b + 3)
                tt_(gt[:, 4:5], gt[:, 1:2], gt[:, 3:4], MUL).then_inc(s_gd, 1)
                for u in range(UNITS - 5, UNITS - 3):
                    shared_add(b, u)
                dve.wait_ge(s_mm, 5 * b + 5)
                link(tt_(sc[:, :], ps[:, 0, 8:8 + E], par["g3b"][:, :], ADD))
                s_j = sc[:, :].rearrange("p (a j) -> p a j", a=1).to_broadcast([P, E, E])
                s_e = sc[:, :].rearrange("p (e a) -> p e a", a=1).to_broadcast([P, E, E])
                link(tt_(cmp_a[:, :, :], s_j, s_e, ALU.is_gt))
                link(tt_(cmp_b[:, :, :], s_j, s_e, ALU.is_equal))
                link(tt_(cmp_b[:, :, :], cmp_b[:, :, :], con["before"][:, :].rearrange("p (e j) -> p e j", e=E), MUL))
                link(tt_(cmp_a[:, :, :], cmp_a[:, :, :], cmp_b[:, :, :], ADD))
                link(v.tensor_reduce(rank[:, :], cmp_a[:, :, :], AX.X, ADD))
                over_k = lambda t: t.rearrange("p (a e) -> p a e", a=1).to_broadcast([P, TOPK, E])
                link(tt_(pick[:, :, :], con["slot"][:, :].rearrange("p (k e) -> p k e", k=TOPK), over_k(rank[:, :]),
                         ALU.is_equal))
                link(tt_(picked[:, :, :], pick[:, :, :], over_k(con["index"][:, :]), MUL))
                link(v.tensor_reduce(idxf[:, :], picked[:, :, :], AX.X, ADD))
                ts(idx[:, :], idxf[:, :], float(E - 1), None, ALU.min).then_inc(s_idx, 1)
                link(tt_(picked[:, :, :], pick[:, :, :], over_k(sc[:, :]), MUL))
                link(v.tensor_reduce(val[:, :], picked[:, :, :], AX.X, ADD))
                ts(gt[:, 6:7], val[:, 0:1], -1.0 / TEMPERATURE, None, MUL).then_inc(s_top, 1)
                for u in range(UNITS - 3, UNITS):
                    shared_add(b, u)
                dve.wait_ge(s_exp, b + 1)
                link(v.reciprocal(gt[:, 8:9], gt[:, 7:8]))
                link(ts(gate[:, :], ex[:, :], gt[:, 8:9], None, MUL))
                assert n_chain[0] == GATE_CHAIN, n_chain
                alone(dve)
                with dve.Fori(0, STEPS) as n:
                    for j in range(2):
                        expert_add(b, n * 2 + j)


def kernel(**inputs):
    import concourse.bacc as bacc
    from concourse.bass_utils import run_bass_kernel_spmd

    nc = bacc.Bacc("TRN2", target_bir_lowering=False, num_devices=1)
    arrays = {k: np.ascontiguousarray(a) for k, a in {**laid_out(inputs), **constants()}.items()}
    d = {k: nc.dram_tensor(k, a.shape, mybir.dt.from_np(a.dtype), kind="ExternalInput").ap() for k, a in arrays.items()}
    out = nc.dram_tensor("out", (B, C, H, W), F32, kind="ExternalOutput").ap()
    build(nc, d, out)
    r = run_bass_kernel_spmd(nc, [arrays], core_ids=[0])
    return r.results[0]["out"]
```
